# Optimizing a Trainium2 kernel written in Bass

```python
import numpy as np
import jax
import jax.numpy as jnp

def _softmax(x, axis=-1):
    return jax.nn.softmax(x, axis=axis)

def _gelu(x):
    return jax.nn.gelu(x, approximate=True)

def _silu(x):
    return jax.nn.silu(x)

def _sigmoid(x):
    return jax.nn.sigmoid(x)

def _layernorm(x, axis=-1, eps=1e-05):
    m = jnp.mean(x, axis=axis, keepdims=True)
    v = jnp.var(x, axis=axis, keepdims=True)
    return (x - m) / jnp.sqrt(v + eps)

def _scatter_add(tgt, idx, src, axis=0):
    return tgt.at[idx].add(src)

def _segment_sum(src, seg, n):
    return jax.ops.segment_sum(src, seg, n)
kernel_name = 'mk_hybrid_d1_jaxref_r8_6378d1'

def setup_inputs(seed: int=0):
    np.random.seed(seed)
    _w = jnp.asarray

    def _L0_attn_a_setup():
        import jax, jax.numpy as jnp
        import numpy as np
        HDC_DIM = 512
        N_HEADS = 4
        HEAD_DIM = HDC_DIM // N_HEADS

        def _ste_sign(w):
            alpha = jnp.mean(jnp.abs(w), axis=-1, keepdims=True)
            hard = alpha * jnp.sign(w)
            hard = jnp.where(hard == 0, alpha, hard)
            return jax.lax.stop_gradient(hard - w) + w
        key = jax.random.key(seed)
        kx, kq, kk, kv = jax.random.split(key, 4)
        B, T = (4, 256)
        x = jax.random.normal(kx, (B, T, HDC_DIM), dtype=jnp.float32)
        bv_q = jax.random.normal(kq, (N_HEADS, HEAD_DIM), dtype=jnp.float32) * 0.02
        bv_k = jax.random.normal(kk, (N_HEADS, HEAD_DIM), dtype=jnp.float32) * 0.02
        bv_v = jax.random.normal(kv, (N_HEADS, HEAD_DIM), dtype=jnp.float32) * 0.02
        return {'x': x, 'bv_q': bv_q, 'bv_k': bv_k, 'bv_v': bv_v}
    _L0_attn_a_in = _L0_attn_a_setup()

    def _L0_attn_b_setup():
        import math
        import jax, jax.numpy as jnp
        import numpy as np
        NUM_HEADS = 32
        HIDDEN = 512
        HEAD_DIM = HIDDEN // NUM_HEADS
        NEG_INF = -1e+30

        def _alibi_slopes(n: int) -> jnp.ndarray:
            cp2 = 2 ** math.floor(math.log2(n))
            base = 2.0 ** (-2.0 ** (-(math.log2(cp2) - 3)))
            slopes = base ** np.arange(1, cp2 + 1, dtype=np.float64)
            if cp2 != n:
                extra_base = 2.0 ** (-2.0 ** (-(math.log2(2 * cp2) - 3)))
                rem = min(cp2, n - cp2)
                extra = extra_base ** np.arange(1, 1 + 2 * rem, 2, dtype=np.float64)
                slopes = np.concatenate([slopes, extra])
            return jnp.asarray(slopes, dtype=jnp.float32)
        key = jax.random.key(seed)
        k1, k2, k3 = jax.random.split(key, 3)
        B, S = (2, 256)
        hidden_states = jax.random.normal(k1, (B, S, HIDDEN), dtype=jnp.float32)
        Wqkv = jax.random.normal(k2, (HIDDEN, NUM_HEADS * HEAD_DIM + 2 * HEAD_DIM), dtype=jnp.float32) * 0.02
        Wo = jax.random.normal(k3, (HIDDEN, HIDDEN), dtype=jnp.float32) * 0.02
        return {'hidden_states': hidden_states, 'Wqkv': Wqkv, 'Wo': Wo}
    _L0_attn_b_in = _L0_attn_b_setup()

    def _L0_ffn_setup():
        import jax, jax.numpy as jnp
        import numpy as np

        @jax.custom_vjp
        def ste_sign(w):
            return jnp.sign(w)

        def _ste_fwd(w):
            return (jnp.sign(w), w)

        def _ste_bwd(w, g):
            mask = ((w > -1) & (w < 1)).astype(g.dtype)
            return (g * mask,)
        ste_sign.defvjp(_ste_fwd, _ste_bwd)
        key = jax.random.key(seed)
        k = jax.random.split(key, 6)
        B, S, H, O, E = (4, 256, 512, 512, 8)
        return {'x': jax.random.normal(k[0], (B, S, H), dtype=jnp.float32), 'weight': jax.random.normal(k[1], (O, H), dtype=jnp.float32) * 0.02, 'bias': jax.random.normal(k[2], (O,), dtype=jnp.float32) * 0.02, 'gate_w': jax.random.normal(k[3], (E, H), dtype=jnp.float32) * 0.02, 'in_channel_scale': jax.random.normal(k[4], (E, H), dtype=jnp.float32), 'out_channel_scale': jax.random.normal(k[5], (E, O), dtype=jnp.float32)}
    _L0_ffn_in = _L0_ffn_setup()
    _d = {'L0_attn_a_x': _L0_attn_a_in['x'], 'L0_attn_a_bv_q': _L0_attn_a_in['bv_q'], 'L0_attn_a_bv_k': _L0_attn_a_in['bv_k'], 'L0_attn_a_bv_v': _L0_attn_a_in['bv_v'], 'L0_attn_b_Wqkv': _L0_attn_b_in['Wqkv'], 'L0_attn_b_Wo': _L0_attn_b_in['Wo'], 'L0_ffn_weight': _L0_ffn_in['weight'], 'L0_ffn_bias': _L0_ffn_in['bias'], 'L0_ffn_gate_w': _L0_ffn_in['gate_w'], 'L0_ffn_in_channel_scale': _L0_ffn_in['in_channel_scale'], 'L0_ffn_out_channel_scale': _L0_ffn_in['out_channel_scale']}
    _x0 = _d['L0_attn_a_x']
    _d['L0_attn_a_x'] = jax.random.normal(jax.random.fold_in(jax.random.key(seed), 1), (2, 1024, 512), dtype=_x0.dtype)
    del _x0
    return _d

def reference(L0_attn_a_x, L0_attn_a_bv_q, L0_attn_a_bv_k, L0_attn_a_bv_v, L0_attn_b_Wqkv, L0_attn_b_Wo, L0_ffn_weight, L0_ffn_bias, L0_ffn_gate_w, L0_ffn_in_channel_scale, L0_ffn_out_channel_scale):

    def _L0_attn_a_ref(x, bv_q, bv_k, bv_v):
        import jax, jax.numpy as jnp
        import numpy as np
        HDC_DIM = 512
        N_HEADS = 4
        HEAD_DIM = HDC_DIM // N_HEADS

        def _ste_sign(w):
            alpha = jnp.mean(jnp.abs(w), axis=-1, keepdims=True)
            hard = alpha * jnp.sign(w)
            hard = jnp.where(hard == 0, alpha, hard)
            return jax.lax.stop_gradient(hard - w) + w
        B, T, D = x.shape
        H, HD = (N_HEADS, HEAD_DIM)
        scale = HD ** (-0.5)
        q_bind = _ste_sign(bv_q)
        k_bind = _ste_sign(bv_k)
        v_bind = _ste_sign(bv_v)
        xh = x.reshape(B, T, H, HD)
        Q = xh * q_bind
        K = xh * k_bind
        V = xh * v_bind
        scores = jnp.einsum('bthd,bshd->bhts', Q, K) * scale
        causal = jnp.tril(jnp.ones((T, T), dtype=bool))
        attn = jnp.where(causal, jax.nn.sigmoid(scores * 4.0), 0.0)
        out = jnp.einsum('bhts,bshd->bthd', attn, V)
        return out.reshape(B, T, D)

    def _L0_attn_b_ref(hidden_states, Wqkv, Wo):
        import math
        import jax, jax.numpy as jnp
        import numpy as np
        NUM_HEADS = 32
        HIDDEN = 512
        HEAD_DIM = HIDDEN // NUM_HEADS
        NEG_INF = -1e+30

        def _alibi_slopes(n: int) -> jnp.ndarray:
            cp2 = 2 ** math.floor(math.log2(n))
            base = 2.0 ** (-2.0 ** (-(math.log2(cp2) - 3)))
            slopes = base ** np.arange(1, cp2 + 1, dtype=np.float64)
            if cp2 != n:
                extra_base = 2.0 ** (-2.0 ** (-(math.log2(2 * cp2) - 3)))
                rem = min(cp2, n - cp2)
                extra = extra_base ** np.arange(1, 1 + 2 * rem, 2, dtype=np.float64)
                slopes = np.concatenate([slopes, extra])
            return jnp.asarray(slopes, dtype=jnp.float32)
        B, S, H = hidden_states.shape
        nH, d = (NUM_HEADS, HEAD_DIM)
        scale = d ** (-0.5)
        qkv = hidden_states @ Wqkv
        q = qkv[..., :nH * d].reshape(B, S, nH, d)
        k = qkv[..., nH * d:nH * d + d]
        v = qkv[..., nH * d + d:]
        scores = jnp.einsum('bqhd,bkd->bhqk', q, k) * scale
        pos_q = jnp.arange(S)[:, None]
        pos_k = jnp.arange(S)[None, :]
        slopes = _alibi_slopes(nH)
        alibi = slopes[:, None, None] * (pos_k - pos_q).astype(jnp.float32)
        causal = pos_k <= pos_q
        scores = jnp.where(causal[None, None], scores + alibi[None], NEG_INF)
        probs = jax.nn.softmax(scores, axis=-1)
        attn = jnp.einsum('bhqk,bkd->bqhd', probs, v).reshape(B, S, H)
        return attn @ Wo

    def _L0_ffn_ref(x, weight, bias, gate_w, in_channel_scale, out_channel_scale):
        import jax, jax.numpy as jnp
        import numpy as np

        @jax.custom_vjp
        def ste_sign(w):
            return jnp.sign(w)

        def _ste_fwd(w):
            return (jnp.sign(w), w)

        def _ste_bwd(w, g):
            mask = ((w > -1) & (w < 1)).astype(g.dtype)
            return (g * mask,)
        ste_sign.defvjp(_ste_fwd, _ste_bwd)
        B, S, H = x.shape
        xf = x.reshape(-1, H)
        router_logits = xf @ gate_w.T
        routing = jax.nn.softmax(router_logits.astype(jnp.float32), axis=1).astype(x.dtype)
        in_scale = routing @ in_channel_scale
        out_scale = routing @ out_channel_scale
        wb = ste_sign(weight)
        out = xf * in_scale @ wb.T * out_scale + bias
        return out.reshape(B, S, -1)
    x = L0_attn_a_x
    x = x + _L0_attn_a_ref(_layernorm(x, axis=-1), L0_attn_a_bv_q, L0_attn_a_bv_k, L0_attn_a_bv_v)
    x = x + _L0_ffn_ref(_layernorm(x, axis=-1), L0_ffn_weight, L0_ffn_bias, L0_ffn_gate_w, L0_ffn_in_channel_scale, L0_ffn_out_channel_scale)
    x = x + _L0_attn_b_ref(_layernorm(x, axis=-1), L0_attn_b_Wqkv, L0_attn_b_Wo)
    x = x + _L0_ffn_ref(_layernorm(x, axis=-1), L0_ffn_weight, L0_ffn_bias, L0_ffn_gate_w, L0_ffn_in_channel_scale, L0_ffn_out_channel_scale)
    return x

_drawn_inputs = setup_inputs


def setup_inputs(seed=0):
    import zlib

    import numpy as np

    out = dict(_drawn_inputs(seed))
    spreads = {}
    factors = {'L0_attn_a_bv_q': 24.415,
     'L0_attn_a_bv_k': 23.875,
     'L0_attn_b_Wqkv': 3.28,
     'L0_attn_b_Wo': 3.368,
     'L0_ffn_bias': 7.441}
    for name, (base, spread) in spreads.items():
        noise = np.random.default_rng([zlib.crc32(name.encode()), seed]).standard_normal(out[name].shape)
        drawn = base * np.exp(spread * noise) if base else spread * noise
        out[name] = jnp.asarray(drawn.astype(out[name].dtype))
    for name, factor in factors.items():
        out[name] = (out[name] * factor).astype(out[name].dtype)
    return out
```

```python
from contextlib import ExitStack

import numpy as np

import concourse.bass as bass
import concourse.mybir as mybir

F32 = mybir.dt.float32
F32R = mybir.dt.float32r
BF16 = mybir.dt.bfloat16
ALU = mybir.AluOpType
ACT = mybir.ActivationFunctionType
AX = mybir.AxisListType

B, T, D = 2, 1024, 512
P = 128
NT = T // P
KT = D // P
CH = 512
NC = T // CH
TPC = CH // P
HA = 4
HB, DH = 32, 16
QD = 4
G = HB // QD
QR = P // QD
E = 8
EPS = 1e-5
NEG = -1e30
R_OFF, R_SLOPE, R_MAX = DH, DH + 1, DH + 2
NPAIR = 3
NPB = 6
WORK = G * T + P * (NT * (NT + 1) // 2) + NPB * 2 * CH
LAG = 2


def plan_units():
    units, count = [], {"act": 0, "dve": 0}

    def add(who, kind, *args):
        count[who] += 1
        units.append(dict(kind=kind, args=args, who=who, order=count[who], k=len(units), slot=len(units) % NPAIR))
        return units[-1]

    stages = {}
    for b in range(B):
        s = []
        for h in range(HA):
            for c in range(NC):
                for i in range(0, TPC * (c + 1), 2):
                    s.append(add("act", "sig", h, c, i))
        stages[b, "attn_a"] = s
        stages[b, "ffn0"] = ffn_units(add)
        s = [add("dve", "q", g) for g in range(G)] + [add("act", "k"), add("act", "v")]
        stages[b, "qkv"] = s
        stages[b, "attn_b"] = softmax_events(add)
        stages[b, "ffn1"] = ffn_units(add)
    return units, stages


def ffn_units(add):
    s = [add("dve", "logits"), add("act", "rT")]
    for c in range(NC):
        s += [add("dve", "ins", c, kp) for kp in range(KT // 2)]
        s += [add("dve", "out", t) for t in range(TPC * c, TPC * c + TPC)]
    return s


def softmax_events(add):
    ev = []

    def max_units(qt):
        return [("unit", "max", qt, c, g, jp) for c in range(qt // TPC + 1) for g in range(G) for jp in range(2)]

    first = max_units(0) + [("unit", "mt", 0)] + max_units(1) + [("unit", "mt", 1)]
    waiting = []
    for qt in range(NT):
        main = [(half, kt) for half in range(2) for kt in range(qt + 1)]
        ahead = max_units(qt + 2) + [("unit", "mt", qt + 2)] if qt + 2 < NT else []
        if qt == 0:
            ev += first
        done = 0
        for n, (half, kt) in enumerate(main):
            ev += [("unit", "exp", qt, half, kt, jp) for jp in range(2)]
            upto = len(ahead) * (n + 1) // len(main)
            ev += ahead[done:upto]
            done = upto
            waiting.append((qt, half, kt))
            if len(waiting) > LAG:
                q2, h2, k2 = waiting.pop(0)
                ev.append(("pv", q2, h2, k2))
                ev += after(q2, h2, k2)
    for q2, h2, k2 in waiting:
        ev.append(("pv", q2, h2, k2))
        ev += after(q2, h2, k2)
    ev = put_off(ev)
    out = []
    for e in ev:
        if e[0] == "unit":
            kind = e[1]
            who = "act" if kind == "exp" else "dve"
            out.append(("unit", add(who, kind, *e[2:])))
        else:
            out.append(e)
    return out


def after(qt, half, kt):
    if kt < qt:
        return []
    return [("late", 1, ("unit", "ot", qt, half))] + ([("late", 2, ("unit", "tt", qt)), ("late", 3, ("unit", "wo", qt))] if half == 1 else [])


def put_off(ev):
    out, late = [], []
    for e in ev:
        if e[0] == "late":
            late.append([e[1], e[2]])
            continue
        out.append(e)
        if e[0] == "pv":
            for x in late:
                x[0] -= 1
            out += [x[1] for x in late if x[0] <= 0]
            late = [x for x in late if x[0] > 0]
    return out + [x[1] for x in late]


def build(nc, x_in, bv_q, bv_k, bv_v, wqkv_in, wo_in, w_in, bias_in, gate_in, ics_in, ocs_in, cq_in, ramp_in, out):
    units, stages = plan_units()

    with ExitStack() as ctx:
        def sb(name, shape, dt=F32):
            return ctx.enter_context(nc.sbuf_tensor(name, shape, dt))

        def psum(name, shape, dt=F32):
            return ctx.enter_context(nc.psum_tensor(name, shape, dt))

        def sem(name):
            return ctx.enter_context(nc.semaphore(name))

        x = sb("x", [P, NT, D])
        xn = sb("xn", [P, NT, D])
        xnT = sb("xnT", [P, KT, T])
        work = sb("work", [P, WORK])
        h_hi = sb("h_hi", [P, KT, CH], F32R)
        h_lo = sb("h_lo", [P, KT, CH], F32R)
        wqkv = sb("wqkv", [P, KT, HB * DH + 2 * DH])
        wq = sb("wq", [P, KT, G, QD, QR])
        wk = sb("wk", [P, KT, QD, QR])
        wo = sb("wo", [P, KT, D])
        wT = sb("wT", [P, KT, D], F32R)
        ics = sb("ics", [E, D])
        ocs = sb("ocs", [E, D])
        gateT = sb("gateT", [P, KT, E])
        bias_bc = sb("bias_bc", [P, D])
        vbc = sb("vbc", [P, D])
        wqk = sb("wqk", [P, HA])
        cq = sb("cq", [P, G, P])
        ramp = sb("ramp", [P, T])
        alpha = sb("alpha", [HA, 3])
        alpham = sb("alpham", [HA, 3])
        ones1 = sb("ones1", [1, P])
        ident = sb("ident", [P, P])
        identb = sb("identb", [P, P], BF16)
        negtri = sb("negtri", [P, P], BF16)
        negtriT = sb("negtriT", [P, P], BF16)
        neghalf = sb("neghalf", [P, NT])
        st = sb("st", [P, NT, 6])
        mv = sb("mv", [P, NT, 2])
        ve = sb("ve", [P, NT])
        rstd = sb("rstd", [P, NT])
        lmax = sb("lmax", [P, NT])
        lsub = sb("lsub", [P, NT, E])
        lexp = sb("lexp", [P, NT, E])
        lsum = sb("lsum", [P, NT])
        lrec = sb("lrec", [P, NT])
        rt = sb("rt", [P, NT, E])
        rT = sb("rT", [E, T])
        vb = sb("vb", [P, NT, QR])
        mx = sb("mx", [P, 2, 2, HB])
        nmx = sb("nmx", [P, 2, HB])
        mT = sb("mT", [HB, 2, P])
        rec = sb("rec", [P, 2, G // 2, QD])

        def area(at, *shape):
            n = int(np.prod(shape))
            names = "abcd"[:len(shape)]
            v = work[:, at:at + n]
            if len(shape) > 1:
                v = v.rearrange(f"p ({' '.join(names)}) -> p {' '.join(names)}", **dict(zip(names[1:], shape[1:])))
            return v

        qT = area(0, HA, T)
        aw = area(HA * T, 2, 2 * TPC, CH)
        va = area(HA * T + 2 * 2 * TPC * CH, NT, D)
        hf = area(0, 2, 2, CH)
        osb = area(4 * CH, 2, D)
        tmp = area(4 * CH + 2 * D, 2, D)
        wraw = area(0, KT, D)
        wsg = area(KT * D, KT, D)
        at = 2 * KT * D
        bv, hard, bsg, bdf, bnd = (area(at + 3 * P * i, 3, P)[0:HA] for i in range(5))
        at += 15 * P
        qks = area(at, P)[0:HA]
        sel = area(at + P, HA, P)[0:HA]
        gate = area(at + P + D, D)[0:E]
        bias1 = area(at + P + 2 * D, D)[0:1]
        qstk = area(0, G, T)
        kst_at = [G * T + P * (q * (q + 1) // 2) for q in range(NT)]
        kst = [work[:, kst_at[q]:kst_at[q] + P * (q + 1)] for q in range(NT)]
        at = G * T + P * (NT * (NT + 1) // 2)
        pb = area(at, NPB, 2, CH)
        at += NPB * 2 * CH
        otS = xn[:, 0:2, :]
        attT = xn[:, 2:4, :]
        att = xn[:, 6:8, :]
        kraw = xn[:, 4:6, :].rearrange("p a b -> p (a b)")
        assert at == WORK

        pair = [psum(f"pair{i}", [P, 2, CH]) for i in range(NPAIR)]
        aux = [psum(f"aux{i}", [P, CH]) for i in range(2)]

        w_in_sem = sem("w_in_sem")
        x_loaded = [sem(f"x_loaded{i}") for i in range(NT // 2)]
        bind_loaded = sem("bind_loaded")
        small_loaded = sem("small_loaded")
        big_loaded = sem("big_loaded")
        stored = [sem(f"stored{i}") for i in range(NT // 2)]
        const_ready = sem("const_ready")
        bind_step = sem("bind_step")
        setup_pe = sem("setup_pe")
        setup_out = sem("setup_out")
        sign_ready = sem("sign_ready")
        pads_ready = sem("pads_ready")
        filled = sem("filled")
        act_took = sem("act_took")
        dve_took = sem("dve_took")
        took = {"act": act_took, "dve": dve_took}
        ln_stats = sem("ln_stats")
        ln_aggr = sem("ln_aggr")
        ln_var = sem("ln_var")
        ln_rstd = sem("ln_rstd")
        xn_ready = sem("xn_ready")
        xn_turned = sem("xn_turned")
        xnT_ready = sem("xnT_ready")
        va_ready = sem("va_ready")
        qT_ready = sem("qT_ready")
        aw_masked = sem("aw_masked")
        av_done = sem("av_done")
        xa_added = sem("xa_added")
        biased = sem("biased")
        soft_step = sem("soft_step")
        exp_ready = sem("exp_ready")
        hi_ready = sem("hi_ready")
        lo_ready = sem("lo_ready")
        os_ready = sem("os_ready")
        xf_added = sem("xf_added")
        kst_ready = sem("kst_ready")
        max_part = sem("max_part")
        max_ready = sem("max_ready")
        max_moved = [sem(f"max_moved{i}") for i in range(2)]
        pv_done = sem("pv_done")
        ot_ready = sem("ot_ready")
        rec_ready = sem("rec_ready")

        block = ctx.enter_context(nc.Block())

        FFN_IN = KT
        LN = 4

        def took_at(u):
            return took[u["who"]], u["order"]

        def pairs_of(b, stage, kind):
            s = stages[b, stage]
            us = [e[1] if isinstance(e, tuple) else e for e in s if not isinstance(e, tuple) or e[0] == "unit"]
            return [u for u in us if u["kind"] == kind]

        exp_units = {(b,) + u["args"]: u for b in range(B) for u in pairs_of(b, "attn_b", "exp")}
        mt_units = {(b,) + u["args"]: u for b in range(B) for u in pairs_of(b, "attn_b", "mt")}
        ot_units = {(b,) + u["args"]: u for b in range(B) for u in pairs_of(b, "attn_b", "ot")}
        tt_units = {(b,) + u["args"]: u for b in range(B) for u in pairs_of(b, "attn_b", "tt")}
        wo_units = {(b,) + u["args"]: u for b in range(B) for u in pairs_of(b, "attn_b", "wo")}
        max_last = {(b, u["args"][0]): u for b in range(B) for u in pairs_of(b, "attn_b", "max")}
        exp_list = {b: pairs_of(b, "attn_b", "exp") for b in range(B)}
        PV_PER = sum(2 * (q + 1) for q in range(NT))

        def pv_index(b, qt, half, kt):
            return b * PV_PER + qt * (qt + 1) + half * (qt + 1) + kt

        def diag_widths(c, i):
            return max(i * P - c * CH, 0)

        @block.sync
        def _(eng):
            xv = x_in.rearrange("b (t p) d -> b p t d", p=P)
            ov = out.rearrange("b (t p) d -> b p t d", p=P)
            for b in range(B):
                for t in range(0, NT, 2):
                    if b > 0:
                        eng.wait_ge(stored[t // 2], 16 * b)
                    eng.dma_start(x[:, t:t + 2, :], xv[b, :, t:t + 2, :]).then_inc(x_loaded[t // 2], 16)
                for qt in range(NT):
                    eng.wait_ge(*took_at(mt_units[b, qt]))
                    for j in range(QD):
                        eng.dma_start(qstk[j * QR + R_MAX:j * QR + R_MAX + 1, :, qt * P:(qt + 1) * P],
                                      mT[j * G:(j + 1) * G, qt % 2, :]).then_inc(max_moved[qt % 2], 16)
                for t in range(0, NT, 2):
                    eng.wait_ge(xf_added, (2 * b + 1) * NT + t + 2)
                    eng.dma_start(ov[b, :, t:t + 2, :], x[:, t:t + 2, :]).then_inc(stored[t // 2], 16)
            for done in stored:
                eng.wait_ge(done, 16 * B)

        @block.gpsimd
        def _(eng):
            eng.memset(ident[:, :], 0.0).then_inc(const_ready, 1)
            eng.memset(sel[:, :, :], 0.0).then_inc(const_ready, 1)
            eng.memset(negtri[:, :], 0.0).then_inc(const_ready, 1)
            eng.memset(negtriT[:, :], 0.0).then_inc(const_ready, 1)
            eng.memset(ones1[:, :], 1.0).then_inc(const_ready, 1)
            eng.memset(neghalf[:, :], -0.5).then_inc(const_ready, 1)
            eng.wait_ge(const_ready, 6)
            eng.affine_select(out=ident[:, :], in_=ident[:, :], compare_op=ALU.not_equal, fill=1.0,
                              base=0, pattern=[[-1, P]], channel_multiplier=1).then_inc(const_ready, 1)
            eng.affine_select(out=sel[:, :, :], in_=sel[:, :, :], compare_op=ALU.not_equal, fill=1.0,
                              base=0, pattern=[[-1, HA], [0, P]], channel_multiplier=1).then_inc(const_ready, 1)
            eng.affine_select(out=negtri[:, :], in_=negtri[:, :], compare_op=ALU.is_ge, fill=NEG,
                              base=0, pattern=[[-1, P]], channel_multiplier=1).then_inc(const_ready, 1)
            eng.affine_select(out=negtriT[:, :], in_=negtriT[:, :], compare_op=ALU.is_ge, fill=NEG,
                              base=0, pattern=[[1, P]], channel_multiplier=-1).then_inc(const_ready, 1)
            eng.wait_ge(const_ready, 10)
            eng.tensor_copy(identb[:, :], ident[:, :]).then_inc(const_ready, 1)
            eng.memset(wq[:, :, :, :, :], 0.0).then_inc(pads_ready, 1)
            eng.memset(wk[:, :, :, :], 0.0).then_inc(pads_ready, 1)
            eng.memset(vb[:, :, :], 0.0).then_inc(pads_ready, 1)
            eng.wait_ge(pads_ready, 3)
            eng.memset(vb[:, :, DH:DH + 1], 1.0).then_inc(pads_ready, 1)

            def pad_weights():
                eng.wait_ge(big_loaded, 64)
                for kt in range(KT):
                    eng.tensor_copy(wq[:, kt, :, :, 0:DH],
                                    wqkv[:, kt, 0:HB * DH].rearrange("p (g j d) -> p g j d", g=G, j=QD)
                                    ).then_inc(pads_ready, 1)
                    for j in range(QD):
                        eng.tensor_copy(wk[:, kt, j, 0:DH], wqkv[:, kt, HB * DH:HB * DH + DH]
                                        ).then_inc(pads_ready, 1)

            for b in range(B):
                for l in range(LN):
                    n = LN * b + l
                    eng.wait_ge(ln_var, n + 1)
                    eng.tensor_tensor(rstd[:, :], ve[:, :], neghalf[:, :], ALU.pow).then_inc(ln_rstd, 1)
                    if l == 0:
                        eng.wait_ge(setup_out, 2)
                        for t in range(NT):
                            eng.wait_ge(xn_ready, n * NT + t + 1)
                            eng.tensor_tensor(va[:, t, :], xn[:, t, :], vbc[:, :], ALU.mult).then_inc(va_ready, 1)
                        if b == 0:
                            pad_weights()
                        for m, (h, c) in enumerate((h, c) for h in range(HA) for c in range(NC)):
                            for u in pairs_of(b, "attn_a", "sig"):
                                if u["args"][:2] != (h, c):
                                    continue
                                for i in (u["args"][2], u["args"][2] + 1):
                                    if i < TPC * c:
                                        continue
                                    w = diag_widths(c, i)
                                    blk = aw[:, (b * HA * NC + m) % 2, i, w:w + P]
                                    eng.wait_ge(act_took, u["order"])
                                    eng.affine_select(out=blk, in_=blk, compare_op=ALU.is_ge, fill=0.0, base=0,
                                                      pattern=[[1, P]], channel_multiplier=-1).then_inc(aw_masked, 1)
                    if l in (1, 3):
                        f = 2 * b + l // 2
                        for t in range(NT):
                            eng.wait_ge(xn_ready, n * NT + t + 1)
                            if f == 0 and t == 0:
                                eng.wait_ge(setup_out, 3)
                            eng.tensor_tensor(x[:, t, :], x[:, t, :], bias_bc[:, :], ALU.add).then_inc(biased, 1)
                    if l == 2:
                        eng.wait_ge(*took_at(pairs_of(b, "qkv", "k")[0]))
                        eng.wait_ge(big_loaded, 64)
                        for q in range(NT):
                            n_k = P * (q + 1)
                            eng.tensor_tensor(kst[q], kraw[:, 0:n_k], ramp[:, T - n_k:T], ALU.add
                                              ).then_inc(kst_ready, 1)

        @block.scalar
        def _(eng):
            eng.dma_start(bv[:, 0, :], bv_q).then_inc(bind_loaded, 16)
            eng.dma_start(bv[:, 1, :], bv_k).then_inc(bind_loaded, 16)
            eng.dma_start(bv[:, 2, :], bv_v).then_inc(bind_loaded, 16)
            eng.dma_start(gate[:, :], gate_in).then_inc(small_loaded, 16)
            eng.dma_start(bias1[:, :], bias_in.rearrange("(a n) -> a n", a=1)).then_inc(small_loaded, 16)
            eng.dma_start(ics[:, :], ics_in).then_inc(small_loaded, 16)
            eng.dma_start(ocs[:, :], ocs_in).then_inc(small_loaded, 16)
            eng.dma_start(wraw, w_in.rearrange("(o p) h -> p o h", p=P)).then_inc(w_in_sem, 16)
            eng.dma_start(wqkv[:, :, :], wqkv_in.rearrange("(k p) n -> p k n", p=P)).then_inc(big_loaded, 16)
            eng.dma_start(wo[:, :, :], wo_in.rearrange("(k p) n -> p k n", p=P)).then_inc(big_loaded, 16)
            eng.dma_start(cq[:, :, :], cq_in).then_inc(big_loaded, 16)
            eng.dma_start(ramp[:, :], ramp_in).then_inc(big_loaded, 16)
            eng.wait_ge(w_in_sem, 16)
            eng.activation(wsg, wraw, ACT.Sign).then_inc(sign_ready, 1)

            def turn_in(n):
                for t in range(NT):
                    eng.wait_ge(xn_turned, n * NT + t + 1)
                    eng.activation(xnT[:, :, t * P:(t + 1) * P],
                                   aux[t % 2][:, :].rearrange("p (k q) -> p k q", k=KT), ACT.Copy
                                   ).then_inc(xnT_ready, 1)

            def ffn(b, stage, f):
                s = stages[b, stage]
                eng.wait_ge(soft_step, 4 * f + 2)
                eng.activation(lexp[:, :, :], lsub[:, :, :], ACT.Exp).then_inc(exp_ready, 1)
                for u in s:
                    if u["kind"] == "rT":
                        eng.wait_ge(filled, u["k"] + 1)
                        eng.activation(rT[:, :], pair[u["slot"]][0:E, :, :].rearrange("p a b -> p (a b)"), ACT.Copy
                                       ).then_inc(act_took, 1)
                    if u["kind"] == "ins":
                        c, kp = u["args"]
                        m = 2 * c + kp
                        eng.wait_ge(dve_took, u["order"])
                        if c >= 1 and kp == 0:
                            eng.wait_ge(filled, pairs_of(b, stage, "out")[TPC * c - 1]["k"] + 1)
                        eng.activation(h_hi[:, 2 * kp:2 * kp + 2, :], hf[:, m % 2, :, :], ACT.Copy
                                       ).then_inc(hi_ready, 1)
                    if u["kind"] == "out":
                        t = u["args"][0]
                        eng.wait_ge(filled, u["k"] + 1)
                        if t >= 2:
                            eng.wait_ge(*took_at(pairs_of(b, stage, "out")[t - 2]))
                        eng.activation(osb[:, t % 2, :], pair[u["slot"]][:, 1, :], ACT.Copy).then_inc(os_ready, 1)

            for b in range(B):
                turn_in(LN * b)
                for u in stages[b, "attn_a"]:
                    h, c, i = u["args"]
                    m = b * HA * NC + h * NC + c
                    eng.wait_ge(filled, u["k"] + 1)
                    if m % (HA * NC) >= 2 and i == 0:
                        eng.wait_ge(av_done, m - 1)
                    if i + 1 < TPC * c:
                        eng.activation(aw[:, m % 2, i:i + 2, :], pair[u["slot"]][:, :, :], ACT.Sigmoid
                                       ).then_inc(act_took, 1)
                    else:
                        w0, w1 = diag_widths(c, i), diag_widths(c, i + 1)
                        eng.activation(aw[:, m % 2, i, w0:CH], pair[u["slot"]][:, 0, w0:CH], ACT.Sigmoid)
                        eng.activation(aw[:, m % 2, i + 1, w1:CH], pair[u["slot"]][:, 1, w1:CH], ACT.Sigmoid
                                       ).then_inc(act_took, 1)
                turn_in(LN * b + 1)
                ffn(b, "ffn0", 2 * b)
                turn_in(LN * b + 2)
                for u in stages[b, "qkv"]:
                    if u["kind"] == "k":
                        eng.wait_ge(filled, u["k"] + 1)
                        eng.activation(kraw, pair[u["slot"]][:, :, :].rearrange("p a b -> p (a b)"), ACT.Copy,
                                       scale=float(DH) ** -0.5).then_inc(act_took, 1)
                    if u["kind"] == "v":
                        eng.wait_ge(filled, u["k"] + 1)
                        eng.wait_ge(pads_ready, 4)
                        eng.activation(vb[:, :, 0:DH],
                                       pair[u["slot"]][:, 0, 0:NT * DH].rearrange("p (t d) -> p t d", d=DH),
                                       ACT.Copy).then_inc(act_took, 1)
                for n, u in enumerate(exp_list[b]):
                    eng.wait_ge(filled, u["k"] + 1)
                    if n >= NPB:
                        qt, half, kt, _ = exp_list[b][n - NPB]["args"]
                        eng.wait_ge(pv_done, pv_index(b, qt, half, kt) + 1)
                    eng.activation(pb[:, n % NPB, :, :], pair[u["slot"]][:, :, :], ACT.Exp).then_inc(act_took, 1)
                turn_in(LN * b + 3)
                ffn(b, "ffn1", 2 * b + 1)

        @block.tensor
        def _(eng):
            def room(u):
                if u["k"] >= NPAIR:
                    eng.wait_ge(*took_at(units[u["k"] - NPAIR]))

            def turn(n):
                for t in range(NT):
                    eng.wait_ge(xn_ready, n * NT + t + 1)
                    if t >= 2:
                        eng.wait_ge(xnT_ready, n * NT + t - 1)
                    for kt in range(KT):
                        mm = eng.transpose(aux[t % 2][:, kt * P:(kt + 1) * P], xn[:, t, kt * P:(kt + 1) * P],
                                           ident[:, :])
                    mm.then_inc(xn_turned, 1)

            def ffn(b, stage, f):
                n = LN * b + (1 if stage == "ffn0" else 3)
                for u in stages[b, stage]:
                    room(u)
                    bank = pair[u["slot"]]
                    if u["kind"] == "logits":
                        for t in range(NT):
                            eng.wait_ge(xnT_ready, n * NT + t + 1)
                            for kt in range(KT):
                                mm = eng.matmul(bank[:, 0, t * E:(t + 1) * E], xnT[:, kt, t * P:(t + 1) * P],
                                                gateT[:, kt, :], start=(kt == 0), stop=(kt == KT - 1))
                    elif u["kind"] == "rT":
                        eng.wait_ge(soft_step, 4 * f + 4)
                        for t in range(NT):
                            mm = eng.transpose(bank[0:E, t // TPC, t % TPC * P:(t % TPC + 1) * P], rt[:, t, :],
                                               ident[:, :])
                    elif u["kind"] == "ins":
                        c, kp = u["args"]
                        eng.wait_ge(*took_at(pairs_of(b, stage, "rT")[0]))
                        for i in range(2):
                            k = 2 * kp + i
                            mm = eng.matmul(bank[:, i, :], ics[:, k * P:(k + 1) * P], rT[:, c * CH:(c + 1) * CH],
                                            start=True, stop=True)
                    else:
                        t = u["args"][0]
                        c = t // TPC
                        eng.wait_ge(lo_ready, f * FFN_IN + 2 * c + 2)
                        eng.matmul(bank[:, 1, :], rT[:, t * P:(t + 1) * P], ocs[:, :], start=True, stop=True)
                        parts = [(h, kt) for h in (h_hi, h_lo) for kt in range(KT)]
                        for m, (h, kt) in enumerate(parts):
                            mm = eng.matmul(bank[:, 0, :], h[:, kt, t % TPC * P:(t % TPC + 1) * P], wT[:, kt, :],
                                            start=(m == 0), stop=(m == len(parts) - 1))
                    mm.then_inc(filled, 1)

            eng.wait_ge(const_ready, 11)
            eng.wait_ge(bind_step, 7)
            eng.transpose(aux[0][:, 0:HA], qks[:, :], ident[0:HA, 0:HA]).then_inc(setup_pe, 1)
            for h in range(HA):
                mm = eng.matmul(aux[1][:, h * P:(h + 1) * P], sel[:, h, :], bnd[:, 2, :], start=True, stop=True)
            mm.then_inc(setup_pe, 1)
            eng.wait_ge(small_loaded, 64)
            eng.matmul(pair[0][:, 0, :], ones1[:, :], bias1[:, :], start=True, stop=True).then_inc(setup_pe, 1)
            for kt in range(KT):
                mm = eng.transpose(pair[0][:, 1, kt * E:(kt + 1) * E], gate[:, kt * P:(kt + 1) * P], ident[0:E, 0:E])
            mm.then_inc(setup_pe, 1)
            eng.wait_ge(sign_ready, 1)
            for kt in range(KT):
                for o in range(KT):
                    mm = eng.transpose(pair[1 + kt // 2][:, kt % 2, o * P:(o + 1) * P], wsg[:, o, kt * P:(kt + 1) * P],
                                       ident[:, :])
                mm.then_inc(setup_pe, 1)
            eng.wait_ge(setup_out, 4 + KT)

            for b in range(B):
                turn(LN * b)
                us = stages[b, "attn_a"]

                def weigh(m):
                    h, c = divmod(m, NC)
                    n = b * HA * NC + m
                    last = [u for u in us if u["args"][:2] == (h, c)][-1]
                    eng.wait_ge(act_took, last["order"])
                    eng.wait_ge(aw_masked, TPC * (n + 1))
                    eng.wait_ge(va_ready, NT * (b + 1))
                    if n % (HA * NC) >= 2:
                        eng.wait_ge(xa_added, n - 1)
                    for t in range(TPC * c, TPC * c + TPC):
                        lo = (t - TPC * c) * P
                        for i in range(t + 1):
                            mm = eng.matmul(aux[n % 2][:, lo:lo + P], aw[:, n % 2, i, lo:lo + P],
                                            va[:, i, h * P:(h + 1) * P], start=(i == 0), stop=(i == t))
                    mm.then_inc(av_done, 1)

                eng.wait_ge(xnT_ready, (LN * b + 1) * NT)
                for u in us:
                    h, c, i0 = u["args"]
                    m = h * NC + c
                    room(u)
                    eng.wait_ge(qT_ready, b * HA + h + 1)
                    for i in (i0, i0 + 1):
                        w = diag_widths(c, i)
                        mm = eng.matmul(pair[u["slot"]][:, i - i0, w:CH], xnT[:, h, i * P:(i + 1) * P],
                                        qT[:, h, c * CH + w:(c + 1) * CH], start=True, stop=True)
                    mm.then_inc(filled, 1)
                    if i0 + 2 == TPC * (c + 1) and m >= 1:
                        weigh(m - 1)
                weigh(HA * NC - 1)

                turn(LN * b + 1)
                ffn(b, "ffn0", 2 * b)

                turn(LN * b + 2)
                eng.wait_ge(xnT_ready, (LN * b + 3) * NT)
                eng.wait_ge(pads_ready, 4 + KT * (1 + QD))
                for u in stages[b, "qkv"]:
                    room(u)
                    bank = pair[u["slot"]]
                    if u["kind"] == "v":
                        for t in range(NT):
                            for kt in range(KT):
                                mm = eng.matmul(bank[:, 0, t * DH:(t + 1) * DH], xnT[:, kt, t * P:(t + 1) * P],
                                                wqkv[:, kt, HB * DH + DH:HB * DH + 2 * DH],
                                                start=(kt == 0), stop=(kt == KT - 1))
                    else:
                        for c in range(NC):
                            for kt in range(KT):
                                w = wq[:, kt, u["args"][0], :, :] if u["kind"] == "q" else wk[:, kt, :, :]
                                mm = eng.matmul(bank[:, c, :], w.rearrange("p j d -> p (j d)"),
                                                xnT[:, kt, c * CH:(c + 1) * CH],
                                                start=(kt == 0), stop=(kt == KT - 1))
                    mm.then_inc(filled, 1)

                eng.wait_ge(*took_at(pairs_of(b, "qkv", "q")[-1]))
                eng.wait_ge(*took_at(pairs_of(b, "qkv", "v")[-1]))
                for e in stages[b, "attn_b"]:
                    if e[0] == "pv":
                        _, qt, half, kt = e
                        n = pv_index(b, qt, half, kt)
                        if kt == 0 and qt * 2 + half >= 2:
                            eng.wait_ge(ot_ready, (b * NT + qt) * 2 + half - 1)
                        for jp in range(2):
                            u = exp_units[b, qt, half, kt, jp]
                            eng.wait_ge(act_took, u["order"])
                            for i in range(2):
                                j = 2 * jp + i
                                mm = eng.matmul(aux[half][j * QR:(j + 1) * QR, :], vb[:, kt, :],
                                                pb[:, exp_list[b].index(u) % NPB, i, :], start=(kt == 0), stop=(kt == qt),
                                                tile_position=(0, j * QR))
                        mm.then_inc(pv_done, 1)
                        continue
                    u = e[1]
                    bank = pair[u["slot"]]
                    room(u)
                    if u["kind"] == "max":
                        qt, c, g, jp = u["args"]
                        w = min(CH, (qt + 1) * P - c * CH)
                        diag = c == qt // TPC
                        eng.wait_ge(kst_ready, b * NT + qt + 1)
                        for i in range(2):
                            r = (2 * jp + i) * QR
                            mm = eng.matmul(bank[:, i, 0:w], qstk[r:r + R_MAX, g, qt * P:(qt + 1) * P],
                                            kst[qt][r:r + R_MAX, c * CH:c * CH + w], start=True, stop=not diag,
                                            tile_position=(r, 0))
                        if diag:
                            for i in range(2):
                                mm = eng.matmul(bank[:, i, w - P:w], identb[:, :], negtri[:, :], start=False, stop=True)
                    elif u["kind"] == "mt":
                        qt = u["args"][0]
                        if qt < TPC:
                            eng.wait_ge(*took_at(max_last[b, qt]))
                        else:
                            eng.wait_ge(max_ready, b * (NT - TPC) + qt - TPC + 1)
                        mm = eng.transpose(bank[0:HB, 0, 0:P], nmx[:, qt % 2, :], ident[:, :])
                    elif u["kind"] == "exp":
                        qt, half, kt, jp = u["args"]
                        eng.wait_ge(max_moved[qt % 2], 16 * QD * ((b * NT + qt) // 2 + 1))
                        for i in range(2):
                            r = (2 * jp + i) * QR
                            mm = eng.matmul(bank[:, i, :], kst[qt][r:r + R_MAX + 1, kt * P:(kt + 1) * P],
                                            qstk[r:r + R_MAX + 1, 4 * half:4 * half + 4, qt * P:(qt + 1) * P],
                                            start=True, stop=kt < qt, tile_position=(r, 0))
                        if kt == qt:
                            for i in range(2):
                                mm = eng.matmul(bank[:, i, :], identb[:, :],
                                                negtriT[:, :].unsqueeze(1).to_broadcast([P, G // 2, P]),
                                                start=False, stop=True)
                    elif u["kind"] == "ot":
                        qt, half = u["args"]
                        eng.wait_ge(ot_ready, (b * NT + qt) * 2 + half + 1)
                        for g in range(G // 2):
                            mm = eng.transpose(bank[:, 0, g * P:(g + 1) * P], otS[:, half, g * P:(g + 1) * P], ident[:, :])
                    elif u["kind"] == "tt":
                        qt = u["args"][0]
                        eng.wait_ge(*took_at(ot_units[b, qt, 1]))
                        for kt in range(KT):
                            mm = eng.transpose(bank[:, 0, kt * P:(kt + 1) * P], att[:, qt % 2, kt * P:(kt + 1) * P],
                                               ident[:, :])
                    else:
                        qt = u["args"][0]
                        eng.wait_ge(*took_at(tt_units[b, qt]))
                        for kt in range(KT):
                            mm = eng.matmul(bank[:, 0, :], attT[:, qt % 2, kt * P:(kt + 1) * P], wo[:, kt, :],
                                            start=(kt == 0), stop=(kt == KT - 1))
                    mm.then_inc(filled, 1)

                turn(LN * b + 3)
                ffn(b, "ffn1", 2 * b + 1)

        @block.vector
        def _(eng):
            eng.wait_ge(bind_loaded, 48)
            eng.tensor_reduce(alpha[:, :], bv[:, :, :], AX.X, ALU.add, apply_absolute_value=True).then_inc(bind_step, 1)
            eng.tensor_scalar(bsg[:, :, :], bv[:, :, :], 0.0, 2.0, ALU.is_ge, ALU.mult).then_inc(bind_step, 1)
            eng.wait_ge(bind_step, 2)
            eng.tensor_scalar(alpham[:, :], alpha[:, :], 1.0 / P, None, ALU.mult).then_inc(bind_step, 1)
            eng.wait_ge(bind_step, 3)
            eng.scalar_tensor_tensor(out=hard[:, :, :], in0=bsg[:, :, :], scalar=-1.0,
                                     in1=alpham[:, :].unsqueeze(2).to_broadcast([HA, 3, P]),
                                     op0=ALU.add, op1=ALU.mult).then_inc(bind_step, 1)
            eng.wait_ge(bind_step, 4)
            eng.tensor_tensor(bdf[:, :, :], hard[:, :, :], bv[:, :, :], ALU.subtract).then_inc(bind_step, 1)
            eng.wait_ge(bind_step, 5)
            eng.tensor_tensor(bnd[:, :, :], bdf[:, :, :], bv[:, :, :], ALU.add).then_inc(bind_step, 1)
            eng.wait_ge(bind_step, 6)
            eng.scalar_tensor_tensor(out=qks[:, :], in0=bnd[:, 0, :], scalar=4.0 * float(P) ** -0.5,
                                     in1=bnd[:, 1, :], op0=ALU.mult, op1=ALU.mult).then_inc(bind_step, 1)
            eng.wait_ge(setup_pe, 1)
            eng.tensor_copy(wqk[:, :], aux[0][:, 0:HA]).then_inc(setup_out, 1)
            eng.wait_ge(setup_pe, 2)
            eng.tensor_copy(vbc[:, :], aux[1][:, :]).then_inc(setup_out, 1)
            eng.wait_ge(setup_pe, 4)
            eng.tensor_copy(bias_bc[:, :], pair[0][:, 0, :]).then_inc(setup_out, 1)
            eng.tensor_copy(gateT[:, :, :], pair[0][:, 1, 0:KT * E].rearrange("p (k e) -> p k e", e=E)
                            ).then_inc(setup_out, 1)
            for kt in range(KT):
                eng.wait_ge(setup_pe, 5 + kt)
                eng.tensor_copy(wT[:, kt, :], pair[1 + kt // 2][:, kt % 2, :]).then_inc(setup_out, 1)

            def norm(n, ready):
                for t in range(NT):
                    ready(t)
                    eng.bn_stats(st[:, t, :], x[:, t, :]).then_inc(ln_stats, 1)
                for t in range(NT):
                    eng.wait_ge(ln_stats, n * NT + t + 1)
                    eng.bn_aggr(mv[:, t, :], st[:, t, :]).then_inc(ln_aggr, 1)
                eng.wait_ge(ln_aggr, (n + 1) * NT)
                eng.tensor_scalar(ve[:, :], mv[:, :, 1], EPS, None, ALU.add).then_inc(ln_var, 1)
                eng.wait_ge(ln_rstd, n + 1)
                for t in range(NT):
                    eng.tensor_scalar(xn[:, t, :], x[:, t, :], mv[:, t, 0:1], rstd[:, t:t + 1],
                                      ALU.subtract, ALU.mult).then_inc(xn_ready, 1)

            def ffn(b, stage, f):
                for u in stages[b, stage]:
                    bank = pair[u["slot"]]
                    if u["kind"] == "logits":
                        lg = bank[:, 0, 0:NT * E].rearrange("p (t e) -> p t e", e=E)
                        eng.wait_ge(filled, u["k"] + 1)
                        eng.tensor_reduce(lmax[:, :], lg, AX.X, ALU.max).then_inc(soft_step, 1)
                        eng.wait_ge(soft_step, 4 * f + 1)
                        eng.tensor_tensor(lsub[:, :, :], lg, lmax[:, :].unsqueeze(2).to_broadcast([P, NT, E]),
                                          ALU.subtract).then_inc(soft_step, 1)
                        eng.wait_ge(soft_step, 4 * f + 2)
                        eng.wait_ge(exp_ready, f + 1)
                        eng.tensor_reduce(lsum[:, :], lexp[:, :, :], AX.X, ALU.add).then_inc(dve_took, 1)
                        eng.wait_ge(dve_took, u["order"])
                        eng.reciprocal(lrec[:, :], lsum[:, :]).then_inc(soft_step, 1)
                        eng.wait_ge(soft_step, 4 * f + 3)
                        eng.tensor_tensor(rt[:, :, :], lexp[:, :, :], lrec[:, :].unsqueeze(2).to_broadcast([P, NT, E]),
                                          ALU.mult).then_inc(soft_step, 1)
                    if u["kind"] == "ins":
                        c, kp = u["args"]
                        m = 2 * c + kp
                        eng.wait_ge(filled, u["k"] + 1)
                        if m >= 2:
                            eng.wait_ge(hi_ready, f * FFN_IN + m - 1)
                            eng.wait_ge(lo_ready, f * FFN_IN + m - 1)
                        eng.tensor_tensor(hf[:, m % 2, :, :], bank[:, :, :],
                                          xnT[:, 2 * kp:2 * kp + 2, c * CH:(c + 1) * CH], ALU.mult
                                          ).then_inc(dve_took, 1)
                        eng.wait_ge(hi_ready, f * FFN_IN + m + 1)
                        eng.tensor_tensor(h_lo[:, 2 * kp:2 * kp + 2, :], hf[:, m % 2, :, :],
                                          h_hi[:, 2 * kp:2 * kp + 2, :].bitcast(F32), ALU.subtract
                                          ).then_inc(lo_ready, 1)
                    if u["kind"] == "out":
                        t = u["args"][0]
                        n = f * NT + t
                        eng.wait_ge(os_ready, n + 1)
                        eng.tensor_tensor(tmp[:, t % 2, :], bank[:, 0, :], osb[:, t % 2, :], ALU.mult
                                          ).then_inc(dve_took, 1)
                        eng.wait_ge(dve_took, u["order"])
                        eng.wait_ge(biased, n + 1)
                        eng.tensor_tensor(x[:, t, :], tmp[:, t % 2, :], x[:, t, :], ALU.add).then_inc(xf_added, 1)

            for b in range(B):
                norm(LN * b, lambda t: eng.wait_ge(x_loaded[t // 2], 16 * (b + 1)))
                for h in range(HA):
                    eng.wait_ge(xnT_ready, (LN * b + 1) * NT)
                    eng.tensor_scalar(qT[:, h, :], xnT[:, h, :], wqk[:, h:h + 1], None, ALU.mult).then_inc(qT_ready, 1)
                for m in range(HA * NC):
                    h, c = divmod(m, NC)
                    n = b * HA * NC + m
                    xs = x[:, TPC * c:TPC * c + TPC, h * P:(h + 1) * P]
                    eng.wait_ge(av_done, n + 1)
                    eng.tensor_tensor(xs, aux[n % 2][:, :].rearrange("p (t q) -> p t q", q=P), xs, ALU.add
                                      ).then_inc(xa_added, 1)
                norm(LN * b + 1, lambda t: eng.wait_ge(xa_added, (b + 1) * HA * NC))
                ffn(b, "ffn0", 2 * b)
                norm(LN * b + 2, lambda t: eng.wait_ge(xf_added, 2 * b * NT + t + 1))
                for u in stages[b, "qkv"]:
                    if u["kind"] == "q":
                        g = u["args"][0]
                        eng.wait_ge(filled, u["k"] + 1)
                        eng.wait_ge(big_loaded, 64)
                        eng.tensor_tensor(qstk[:, g, :].rearrange("p (t q) -> p t q", q=P),
                                          pair[u["slot"]][:, :, :].rearrange("p a (t q) -> p (a t) q", q=P),
                                          cq[:, g, :].unsqueeze(1).to_broadcast([P, NT, P]), ALU.add
                                          ).then_inc(dve_took, 1)
                for e in stages[b, "attn_b"]:
                    if e[0] == "pv":
                        _, qt, half, kt = e
                        if kt == qt:
                            n = (b * NT + qt) * 2 + half
                            eng.wait_ge(pv_done, pv_index(b, qt, half, kt) + 1)
                            if qt > 0:
                                eng.wait_ge(filled, ot_units[b, qt - 1, half]["k"] + 1)
                            eng.tensor_copy(otS[:, half, :], aux[half][:, :]).then_inc(ot_ready, 1)
                        continue
                    u = e[1]
                    bank = pair[u["slot"]]
                    if u["kind"] == "exp":
                        continue
                    eng.wait_ge(filled, u["k"] + 1)
                    if u["kind"] == "max":
                        qt, c, g, jp = u["args"]
                        w = min(CH, (qt + 1) * P - c * CH)
                        o = mx[:, qt % 2, c, :] if qt >= TPC else nmx[:, qt % 2, :]
                        if qt < TPC and qt >= 2 and g == 0 and jp == 0:
                            eng.wait_ge(filled, mt_units[b, qt - 2]["k"] + 1)
                        o = o.rearrange("p (j g) -> p j g", j=QD)[:, 2 * jp:2 * jp + 2, g]
                        ins = eng.tensor_reduce(o, bank[:, :, 0:w], AX.X, ALU.max, negate=True)
                        ins.then_inc(dve_took, 1)
                        if c == qt // TPC and g == G - 1 and jp == 1:
                            eng.wait_ge(dve_took, u["order"])
                            if qt >= TPC:
                                eng.wait_ge(filled, mt_units[b, qt - 2]["k"] + 1)
                                eng.tensor_tensor(nmx[:, qt % 2, :], mx[:, qt % 2, 0, :], mx[:, qt % 2, 1, :], ALU.min
                                                  ).then_inc(max_ready, 1)
                    elif u["kind"] == "mt":
                        qt = u["args"][0]
                        if qt >= 2:
                            eng.wait_ge(max_moved[qt % 2], 16 * QD * ((b * NT + qt) // 2))
                        eng.tensor_copy(mT[:, qt % 2, :], bank[0:HB, 0, 0:P]).then_inc(dve_took, 1)
                    elif u["kind"] == "ot":
                        qt, half = u["args"]
                        o = bank[:, 0, :].rearrange("p (g j d) -> p g j d", g=G // 2, j=QD)
                        eng.reciprocal(rec[:, half, :, :].unsqueeze(3), o[:, :, :, DH:DH + 1]).then_inc(rec_ready, 1)
                        eng.wait_ge(rec_ready, (b * NT + qt) * 2 + half + 1)
                        w = G // 2 * QD
                        dst = att[:, qt % 2, half * w * DH:(half + 1) * w * DH].rearrange("p (g j d) -> p g j d", g=G // 2, j=QD)
                        eng.tensor_tensor(dst, o[:, :, :, 0:DH],
                                          rec[:, half, :, :].unsqueeze(3).to_broadcast([P, G // 2, QD, DH]), ALU.mult
                                          ).then_inc(dve_took, 1)
                    elif u["kind"] == "tt":
                        qt = u["args"][0]
                        eng.tensor_copy(attT[:, qt % 2, :], bank[:, 0, :]).then_inc(dve_took, 1)
                    elif u["kind"] == "wo":
                        qt = u["args"][0]
                        eng.tensor_tensor(x[:, qt, :], bank[:, 0, :], x[:, qt, :], ALU.add).then_inc(dve_took, 1)
                norm(LN * b + 3, lambda t: eng.wait_ge(*took_at(wo_units[b, t])))
                ffn(b, "ffn1", 2 * b + 1)


def constants():
    base = 2.0 ** (-2.0 ** (-(np.log2(HB) - 3)))
    slope = (base ** np.arange(1, HB + 1, dtype=np.float64)).astype(np.float32).astype(np.float64)
    cq = np.zeros((P, G, P), np.float32)
    ramp = np.zeros((P, T), np.float32)
    for j in range(QD):
        for g in range(G):
            cq[j * QR + R_OFF, g, :] = -slope[QD * g + j] * np.arange(P)
            cq[j * QR + R_SLOPE, g, :] = slope[QD * g + j]
        ramp[j * QR + R_OFF, :] = 1.0
        ramp[j * QR + R_SLOPE, :] = np.arange(T) - (T - P)
        ramp[j * QR + R_MAX, :] = 1.0
    return cq, ramp


_INS = ["L0_attn_a_x", "L0_attn_a_bv_q", "L0_attn_a_bv_k", "L0_attn_a_bv_v", "L0_attn_b_Wqkv", "L0_attn_b_Wo",
        "L0_ffn_weight", "L0_ffn_bias", "L0_ffn_gate_w", "L0_ffn_in_channel_scale", "L0_ffn_out_channel_scale"]


def kernel(**inputs):
    import concourse.bacc as _bacc
    from concourse.bass_utils import run_bass_kernel_spmd as _run

    nc = _bacc.Bacc("TRN2", target_bir_lowering=False, num_devices=1)
    arrays = {f"in_{n}_dram": np.ascontiguousarray(inputs[n]) for n in _INS}
    cq, ramp = constants()
    arrays["slope_rows_dram"], arrays["position_rows_dram"] = cq, ramp
    args = [nc.dram_tensor(n, a.shape, mybir.dt.from_np(a.dtype), kind="ExternalInput").ap() for n, a in arrays.items()]
    out = nc.dram_tensor("out_0_dram", (B, T, D), F32, kind="ExternalOutput").ap()
    build(nc, *args, out)
    r = _run(nc, [arrays], core_ids=[0])
    return r.results[0]["out_0_dram"]
```

```python
from contextlib import ExitStack

import numpy as np

import concourse.bass as bass
import concourse.mybir as mybir

F32 = mybir.dt.float32
F32R = mybir.dt.float32r
BF16 = mybir.dt.bfloat16
ALU = mybir.AluOpType
ACT = mybir.ActivationFunctionType
AX = mybir.AxisListType

B, T, D = 2, 1024, 512
P = 128
NT = T // P
KT = D // P
CH = 512
NC = T // CH
TPC = CH // P
HA = 4
HB, DH = 32, 16
HP = P // 2
G = HB // 2
GQ = 4
QR = 32
E = 8
EPS = 1e-5
NEG = -1e30
R_SLOPE, R_OFF, R_MAX = 3 * DH, 3 * DH + 2, 3 * DH + 4
NFIX = HP - R_SLOPE
NQS = 3
RS = 64
NPAIR = 3
NPB = 6
WORK = 2 * HA * T + 4 * TPC * CH
NKST = sum(2 * P * (a + 1) for a in range(NT // 2))
LEAD = 4
MAX_RATE = 3
MOVE_BEHIND = 4
LAG = 2


def plan_units():
    units, count = [], {"act": 0, "dve": 0}

    def add(who, kind, *args):
        count[who] += 1
        units.append(dict(kind=kind, args=args, who=who, order=count[who], k=len(units), slot=len(units) % NPAIR))
        return units[-1]

    stages = {}
    for b in range(B):
        s = []
        for h in range(HA):
            for c in range(NC):
                for i in range(0, TPC * (c + 1), 2):
                    s.append(add("act", "sig", h, c, i))
        stages[b, "attn_a"] = s
        stages[b, "ffn0"] = ffn_units(add)
        s = [add("dve", "q", 0, 0), add("dve", "q", 0, 1), add("act", "k"), add("act", "v"),
             add("dve", "q", 1, 0), add("dve", "q", 1, 1)]
        stages[b, "qkv"] = s
        stages[b, "attn_b"] = softmax_events(add)
        stages[b, "ffn1"] = ffn_units(add)
    return units, stages


def ffn_units(add):
    s = [add("dve", "logits"), add("act", "rT")]
    for c in range(NC):
        s += [add("dve", "ins", c, kp) for kp in range(KT // 2)]
        s += [add("dve", "out", t) for t in range(TPC * c, TPC * c + TPC)]
    return s


def softmax_events(add):
    groups = [(qt, half, kt) for qt in range(NT) for half in range(2) for kt in range(qt + 1)]
    extra = [[] for _ in groups]
    at, room_left = len(groups), 0
    first = []
    for qt in reversed(range(NT)):
        start = qt * (qt + 1) - LEAD
        if at > start:
            at, room_left = start, MAX_RATE
        us = [("mt", qt)] + [("max", qt, c, g) for c in reversed(range(qt // TPC + 1)) for g in reversed(range(G))]
        for u in us:
            if room_left == 0:
                at, room_left = at - 1, MAX_RATE
            (extra[at] if at >= 0 else first).insert(0, ("unit",) + u)
            if u[0] == "max":
                room_left -= 1
    ev = first
    waiting = []
    for n, (qt, half, kt) in enumerate(groups):
        ahead = extra[n]
        ev.append(("unit", "exp", qt, half, kt, 0))
        ev += ahead[:1]
        ev.append(("unit", "exp", qt, half, kt, 1))
        ev += ahead[1:2]
        waiting.append((qt, half, kt))
        if len(waiting) > LAG:
            q2, h2, k2 = waiting.pop(0)
            ev.append(("pv", q2, h2, k2))
            ev += after(q2, h2, k2)
        ev += ahead[2:]
    for q2, h2, k2 in waiting:
        ev.append(("pv", q2, h2, k2))
        ev += after(q2, h2, k2)
    ev = put_off(ev)
    out = []
    for e in ev:
        if e[0] == "unit":
            kind = e[1]
            who = "act" if kind == "exp" else "dve"
            out.append(("unit", add(who, kind, *e[2:])))
        else:
            out.append(e)
    return out


def after(qt, half, kt):
    if kt < qt:
        return []
    return [("late", 1, ("unit", "ot", qt, half))] + ([("late", 2, ("unit", "tt", qt)), ("late", 3, ("unit", "wo", qt))] if half == 1 else [])


def put_off(ev):
    out, late = [], []
    for e in ev:
        if e[0] == "late":
            late.append([e[1], e[2]])
            continue
        out.append(e)
        if e[0] == "pv":
            for x in late:
                x[0] -= 1
            out += [x[1] for x in late if x[0] <= 0]
            late = [x for x in late if x[0] > 0]
    return out + [x[1] for x in late]


def build(nc, x_in, bv_q, bv_k, bv_v, wqkv_in, wo_in, w_in, bias_in, gate_in, ics_in, ocs_in, cq_in, ramp_in, out):
    units, stages = plan_units()

    with ExitStack() as ctx:
        def sb(name, shape, dt=F32):
            return ctx.enter_context(nc.sbuf_tensor(name, shape, dt))

        def psum(name, shape, dt=F32):
            return ctx.enter_context(nc.psum_tensor(name, shape, dt))

        def sem(name):
            return ctx.enter_context(nc.semaphore(name))

        x = sb("x", [P, NT, D])
        xnT = sb("xnT", [P, KT, T])
        h_split = sb("h_split", [P, 2, KT, CH], F32R)
        h_hi, h_lo = h_split[:, 0, :, :], h_split[:, 1, :, :]
        with nc.sbuf_tensor("xn", [P, NT, D], F32) as xn:
            pass
        qT_hi = sb("qT_hi", [P, KT, T], F32R)
        qT_lo = h_split[:, :, :, :].rearrange("p a k n -> p (a k n)").rearrange("p (k t) -> p k t", t=T)
        with nc.sbuf_tensor("work", [P, WORK], F32) as work:
            pass
        qs = sb("qs", [P, NQS, G, 2 * P], F32R)
        pb = sb("pb", [P, NPB, 2, CH])
        kst_all = sb("kst_all", [P, 2, NKST], F32R)
        qs_words = qs[:, :, :, :].bitcast(F32)
        wqkv = sb("wqkv", [P, KT, HB * DH + 2 * DH])
        wk = sb("wk", [P, KT, 2, HP])
        wo = sb("wo", [P, KT, D])
        wT = sb("wT", [P, KT, D], F32R)
        narrow = sb("narrow", [P, T + 2 * D], F32R)
        rT = narrow[0:RS, 0:T]
        scales = narrow[0:RS, T:T + 2 * D].rearrange("r (a n) -> r a n", a=2)
        gateT = sb("gateT", [P, KT, E])
        bias_bc = sb("bias_bc", [P, D])
        vbc = sb("vbc", [P, D])
        wqk = sb("wqk", [P, HA])
        cq = narrow[P - 4 * NFIX:P, :].rearrange("r (g q) -> r g q", q=P)
        ramp = sb("ramp", [P, T])
        alpha = sb("alpha", [HA, 3])
        alpham = sb("alpham", [HA, 3])
        ones1 = sb("ones1", [1, P])
        ident = sb("ident", [P, P])
        identb = sb("identb", [P, P], BF16)
        negtri = sb("negtri", [P, P], BF16)
        negtriT = sb("negtriT", [P, P], BF16)
        neghalf = sb("neghalf", [P, NT])
        st = sb("st", [P, NT, 6])
        mv = sb("mv", [P, NT, 2])
        ve = sb("ve", [P, NT])
        rstd = sb("rstd", [P, NT])
        lmax = sb("lmax", [P, NT])
        lsub = sb("lsub", [P, NT, E])
        lexp = sb("lexp", [P, NT, E])
        lsum = sb("lsum", [P, NT])
        lrec = sb("lrec", [P, NT])
        rt = sb("rt", [P, NT, E])
        rt_hi = sb("rt_hi", [P, NT, E], F32R)
        rstk = sb("rstk", [P, NT, RS])
        vb = sb("vb", [P, NT, QR])
        mx = sb("mx", [P, 2, 2, HB])
        nmx = sb("nmx", [P, 2, HB])
        mT_hi = sb("mT_hi", [HB, 2, P], F32R)
        mT_lo = sb("mT_lo", [HB, 2, P], F32R)
        rec = sb("rec", [P, 2, HB // 2])

        def area(at, *shape):
            n = int(np.prod(shape))
            names = "abcd"[:len(shape)]
            v = work[:, at:at + n]
            if len(shape) > 1:
                v = v.rearrange(f"p ({' '.join(names)}) -> p {' '.join(names)}", **dict(zip(names[1:], shape[1:])))
            return v

        qT = area(0, HA, T)
        aw = area(HA * T, 2, 2 * TPC, CH)
        va = area(HA * T + 2 * 2 * TPC * CH, NT, D)
        hf = area(0, 2, 2, CH)
        osb = area(4 * CH, 2, D)
        tmp = area(4 * CH + 2 * D, 2, D)
        wraw = area(0, KT, D)
        wsg = area(KT * D, KT, D)
        at = 2 * KT * D
        bv, hard, bsg, bdf, bnd = (area(at + 3 * P * i, 3, P)[0:HA] for i in range(5))
        at += 15 * P
        qks = area(at, P)[0:HA]
        sel = area(at + P, HA, P)[0:HA]
        gate = area(at + P + D, D)[0:E]
        bias1 = area(at + P + 2 * D, D)[0:1]
        scale_raw = area(at + P + 3 * D, 2, D)[0:RS]
        scale_lo = area(at + P + 5 * D, 2, D)[0:RS]
        at += 2 * D
        cq_raw = area(at + P + 5 * D, G, P)[P - 4 * NFIX:P]
        assert at + P + 5 * D + G * P <= WORK
        kst = [kst_all[:, :, P * a * (a + 1):P * (a + 1) * (a + 2)] for a in range(NT // 2)]
        keys = pb[:, NPB - 1, :, :].rearrange("p a b -> p (a b)")
        otS = xnT[:, 0, :].rearrange("p (a b) -> p a b", a=2)
        attT = xnT[:, 1, :].rearrange("p (a b) -> p a b", a=2)
        att = xnT[:, 2, :].rearrange("p (a b) -> p a b", a=2)

        pair = [psum(f"pair{i}", [P, 2, CH]) for i in range(NPAIR)]
        aux = [psum(f"aux{i}", [P, CH]) for i in range(2)]

        w_in_sem = sem("w_in_sem")
        x_loaded = [sem(f"x_loaded{i}") for i in range(NT // 2)]
        bind_loaded = sem("bind_loaded")
        small_loaded = sem("small_loaded")
        big_loaded = sem("big_loaded")
        scales_loaded = sem("scales_loaded")
        cq_loaded = sem("cq_loaded")
        cq_ready = sem("cq_ready")
        scales_step = sem("scales_step")
        stored = [sem(f"stored{i}") for i in range(NT // 2)]
        const_ready = sem("const_ready")
        bind_step = sem("bind_step")
        setup_pe = sem("setup_pe")
        setup_out = sem("setup_out")
        sign_ready = sem("sign_ready")
        pads_ready = sem("pads_ready")
        filled = sem("filled")
        act_took = sem("act_took")
        dve_took = sem("dve_took")
        took = {"act": act_took, "dve": dve_took}
        ln_stats = sem("ln_stats")
        ln_aggr = sem("ln_aggr")
        ln_var = sem("ln_var")
        ln_rstd = sem("ln_rstd")
        xn_ready = sem("xn_ready")
        xn_turned = sem("xn_turned")
        xnT_ready = sem("xnT_ready")
        va_ready = sem("va_ready")
        qT_ready = sem("qT_ready")
        aw_masked = sem("aw_masked")
        av_done = sem("av_done")
        xa_added = sem("xa_added")
        biased = sem("biased")
        soft_step = sem("soft_step")
        rt_split = sem("rt_split")
        exp_ready = sem("exp_ready")
        hi_ready = sem("hi_ready")
        lo_ready = sem("lo_ready")
        os_ready = sem("os_ready")
        xf_added = sem("xf_added")
        keys_step = sem("keys_step")
        qT_split = sem("qT_split")
        kst_ready = sem("kst_ready")
        halves_zeroed = sem("halves_zeroed")
        stack_moved = [sem(f"stack_moved{i}") for i in range(NT // 2)]
        max_split = sem("max_split")
        max_ready = sem("max_ready")
        max_moved = [sem(f"max_moved{i}") for i in range(2)]
        pv_done = sem("pv_done")
        ot_ready = sem("ot_ready")
        rec_ready = sem("rec_ready")

        block = ctx.enter_context(nc.Block())

        FFN_IN = KT
        LN = 4

        def took_at(u):
            return took[u["who"]], u["order"]

        def pairs_of(b, stage, kind):
            s = stages[b, stage]
            us = [e[1] if isinstance(e, tuple) else e for e in s if not isinstance(e, tuple) or e[0] == "unit"]
            return [u for u in us if u["kind"] == kind]

        exp_units = {(b,) + u["args"]: u for b in range(B) for u in pairs_of(b, "attn_b", "exp")}
        mt_units = {(b,) + u["args"]: u for b in range(B) for u in pairs_of(b, "attn_b", "mt")}
        ot_units = {(b,) + u["args"]: u for b in range(B) for u in pairs_of(b, "attn_b", "ot")}
        tt_units = {(b,) + u["args"]: u for b in range(B) for u in pairs_of(b, "attn_b", "tt")}
        wo_units = {(b,) + u["args"]: u for b in range(B) for u in pairs_of(b, "attn_b", "wo")}
        max_last = {(b, u["args"][0]): u for b in range(B) for u in pairs_of(b, "attn_b", "max")}
        exp_last = {(b, u["args"][0]): u for b in range(B) for u in pairs_of(b, "attn_b", "exp")}
        exp_list = {b: pairs_of(b, "attn_b", "exp") for b in range(B)}
        PV_PER = sum(2 * (q + 1) for q in range(NT))

        def pv_index(b, qt, half, kt):
            return b * PV_PER + qt * (qt + 1) + half * (qt + 1) + kt

        def diag_widths(c, i):
            return max(i * P - c * CH, 0)

        @block.sync
        def _(eng):
            xv = x_in.rearrange("b (t p) d -> b p t d", p=P)
            ov = out.rearrange("b (t p) d -> b p t d", p=P)
            for b in range(B):
                for t in range(0, NT, 2):
                    if b > 0:
                        eng.wait_ge(stored[t // 2], 16 * b)
                    eng.dma_start(x[:, t:t + 2, :], xv[b, :, t:t + 2, :]).then_inc(x_loaded[t // 2], 16)
                eng.wait_ge(xf_added, (2 * b + 1) * NT)
                if b == 0:
                    eng.wait_ge(cq_ready, 1)

                def move_stack(a):
                    if a % 2 == 0:
                        for u in pairs_of(b, "qkv", "q")[a:a + 2]:
                            eng.wait_ge(*took_at(u))
                    if a >= NQS:
                        eng.wait_ge(filled, exp_last[b, 2 * (a - NQS) + 1]["k"] + 1)
                    for j in range(2):
                        r = j * HP + R_SLOPE
                        for i in range(2):
                            at = (2 * i + j) * NFIX
                            eng.dma_start(qs_words[r:r + NFIX, a % NQS, :, i * P:(i + 1) * P],
                                          cq[at:at + NFIX, :, :].bitcast(F32)).then_inc(stack_moved[a], 16)
                    for hh in range(8):
                        for part, q in enumerate((qT_hi, qT_lo, qT_hi)):
                            r = hh % 2 * HP + part * DH
                            g = hh // 2 * GQ
                            eng.dma_start(qs_words[r:r + DH, a % NQS, g:g + GQ, :],
                                          q[hh * DH:(hh + 1) * DH, :, a * 2 * P:(a + 1) * 2 * P].bitcast(F32)
                                          ).then_inc(stack_moved[a], 16)

                for a in range(NQS):
                    move_stack(a)
                for qt in range(NT):
                    eng.wait_ge(*took_at(mt_units[b, qt]))
                    for j in range(2):
                        for n, m in enumerate((mT_hi, mT_lo)):
                            r = j * HP + R_MAX + n
                            eng.dma_start(qs_words[r:r + 1, qt // 2 % NQS, :, qt % 2 * P:(qt % 2 + 1) * P],
                                          m[j * G:(j + 1) * G, qt % 2, :].bitcast(F32)).then_inc(max_moved[qt % 2], 16)
                    if qt == MOVE_BEHIND:
                        move_stack(NQS)
                for t in range(0, NT, 2):
                    eng.wait_ge(xf_added, (2 * b + 1) * NT + t + 2)
                    eng.dma_start(ov[b, :, t:t + 2, :], x[:, t:t + 2, :]).then_inc(stored[t // 2], 16)
            for done in stored:
                eng.wait_ge(done, 16 * B)

        @block.gpsimd
        def _(eng):
            eng.memset(ident[:, :], 0.0).then_inc(const_ready, 1)
            eng.memset(sel[:, :, :], 0.0).then_inc(const_ready, 1)
            eng.memset(negtri[:, :], 0.0).then_inc(const_ready, 1)
            eng.memset(negtriT[:, :], 0.0).then_inc(const_ready, 1)
            eng.memset(ones1[:, :], 1.0).then_inc(const_ready, 1)
            eng.memset(neghalf[:, :], -0.5).then_inc(const_ready, 1)
            eng.wait_ge(const_ready, 6)
            eng.affine_select(out=ident[:, :], in_=ident[:, :], compare_op=ALU.not_equal, fill=1.0,
                              base=0, pattern=[[-1, P]], channel_multiplier=1).then_inc(const_ready, 1)
            eng.affine_select(out=sel[:, :, :], in_=sel[:, :, :], compare_op=ALU.not_equal, fill=1.0,
                              base=0, pattern=[[-1, HA], [0, P]], channel_multiplier=1).then_inc(const_ready, 1)
            eng.affine_select(out=negtri[:, :], in_=negtri[:, :], compare_op=ALU.is_ge, fill=NEG,
                              base=0, pattern=[[-1, P]], channel_multiplier=1).then_inc(const_ready, 1)
            eng.affine_select(out=negtriT[:, :], in_=negtriT[:, :], compare_op=ALU.is_ge, fill=NEG,
                              base=0, pattern=[[1, P]], channel_multiplier=-1).then_inc(const_ready, 1)
            eng.wait_ge(const_ready, 10)
            eng.tensor_copy(identb[:, :], ident[:, :]).then_inc(const_ready, 1)
            eng.memset(rstk[:, :, :], 0.0).then_inc(pads_ready, 1)
            eng.memset(wk[:, :, :, :], 0.0).then_inc(pads_ready, 1)
            eng.memset(vb[:, :, :], 0.0).then_inc(pads_ready, 1)
            eng.wait_ge(pads_ready, 3)
            eng.memset(vb[:, :, DH:DH + 1], 1.0).then_inc(pads_ready, 1)
            eng.memset(scale_raw, 0.0).then_inc(pads_ready, 1)

            def pad_weights():
                eng.wait_ge(big_loaded, 16 * 11)
                for j in range(2):
                    for part in range(3):
                        eng.tensor_copy(wk[:, :, j, part * DH:(part + 1) * DH], wqkv[:, :, HB * DH:HB * DH + DH]
                                        ).then_inc(pads_ready, 1)

            for b in range(B):
                for l in range(LN):
                    n = LN * b + l
                    eng.wait_ge(ln_var, n + 1)
                    eng.tensor_tensor(rstd[:, :], ve[:, :], neghalf[:, :], ALU.pow).then_inc(ln_rstd, 1)
                    if l == 0:
                        eng.wait_ge(setup_out, 2)
                        for t in range(NT):
                            eng.wait_ge(xn_ready, n * NT + t + 1)
                            eng.tensor_tensor(va[:, t, :], xn[:, t, :], vbc[:, :], ALU.mult).then_inc(va_ready, 1)
                        if b == 0:
                            pad_weights()
                        for m, (h, c) in enumerate((h, c) for h in range(HA) for c in range(NC)):
                            for u in pairs_of(b, "attn_a", "sig"):
                                if u["args"][:2] != (h, c):
                                    continue
                                for i in (u["args"][2], u["args"][2] + 1):
                                    if i < TPC * c:
                                        continue
                                    w = diag_widths(c, i)
                                    blk = aw[:, (b * HA * NC + m) % 2, i, w:w + P]
                                    eng.wait_ge(act_took, u["order"])
                                    eng.affine_select(out=blk, in_=blk, compare_op=ALU.is_ge, fill=0.0, base=0,
                                                      pattern=[[1, P]], channel_multiplier=-1).then_inc(aw_masked, 1)
                    if l in (1, 3):
                        f = 2 * b + l // 2
                        for t in range(NT):
                            eng.wait_ge(xn_ready, n * NT + t + 1)
                            if f == 0 and t == 0:
                                eng.wait_ge(setup_out, 3)
                            eng.tensor_tensor(x[:, t, :], x[:, t, :], bias_bc[:, :], ALU.add).then_inc(biased, 1)
                    if l == 2:
                        eng.wait_ge(keys_step, 4 * b + 4)
                        for a in range(NT // 2):
                            n_k = 2 * P * (a + 1)
                            for j in range(2):
                                r = j * HP
                                eng.tensor_tensor(kst[a][r:r + HP, j, :], keys[r:r + HP, 0:n_k], ramp[r:r + HP, T - n_k:T],
                                                  ALU.add).then_inc(kst_ready, 1)

        @block.scalar
        def _(eng):
            eng.dma_start(bv[:, 0, :], bv_q).then_inc(bind_loaded, 16)
            eng.dma_start(bv[:, 1, :], bv_k).then_inc(bind_loaded, 16)
            eng.dma_start(bv[:, 2, :], bv_v).then_inc(bind_loaded, 16)
            eng.dma_start(gate[:, :], gate_in).then_inc(small_loaded, 16)
            eng.dma_start(bias1[:, :], bias_in.rearrange("(a n) -> a n", a=1)).then_inc(small_loaded, 16)
            eng.wait_ge(pads_ready, 5)
            for r in (0, E, QR, QR + E):
                eng.dma_start(scale_raw[r:r + E, 0, :], ics_in).then_inc(scales_loaded, 16)
                eng.dma_start(scale_raw[r:r + E, 1, :], ocs_in).then_inc(scales_loaded, 16)
            eng.dma_start(cq_raw, cq_in).then_inc(cq_loaded, 16)
            eng.dma_start(wraw, w_in.rearrange("(o p) h -> p o h", p=P)).then_inc(w_in_sem, 16)
            for kt in range(KT):
                for half in range(2):
                    w = wqkv[:, kt, 0:HB * DH].rearrange("p (m h n) -> p m h n", m=KT, h=2)
                    eng.dma_start(w[:, :, half, :],
                                  wqkv_in[kt * P:(kt + 1) * P, half * D // 2:(half + 1) * D // 2]
                                  .rearrange("p (m n) -> p m n", m=KT)).then_inc(big_loaded, 16)
            eng.dma_start(wqkv[:, :, HB * DH:], wqkv_in.rearrange("(k p) n -> p k n", p=P)[:, :, HB * DH:]
                          ).then_inc(big_loaded, 16)
            eng.dma_start(wo[:, :, :], wo_in.rearrange("(k p) n -> p k n", p=P)).then_inc(big_loaded, 16)
            eng.dma_start(ramp[:, :], ramp_in).then_inc(big_loaded, 16)
            eng.wait_ge(w_in_sem, 16)
            eng.activation(wsg, wraw, ACT.Sign).then_inc(sign_ready, 1)

            def turn_in(n):
                for t in range(NT):
                    eng.wait_ge(xn_turned, n * NT + t + 1)
                    eng.activation(xnT[:, :, t * P:(t + 1) * P],
                                   aux[t % 2][:, :].rearrange("p (k q) -> p k q", k=KT), ACT.Copy
                                   ).then_inc(xnT_ready, 1)

            def ffn(b, stage, f):
                s = stages[b, stage]
                eng.wait_ge(soft_step, 6 * f + 2)
                eng.activation(lexp[:, :, :], lsub[:, :, :], ACT.Exp).then_inc(exp_ready, 1)
                for u in s:
                    if u["kind"] == "rT":
                        eng.wait_ge(filled, u["k"] + 1)
                        eng.activation(rT, pair[u["slot"]][0:RS, :, :].rearrange("p a b -> p (a b)"), ACT.Copy
                                       ).then_inc(act_took, 1)
                    if u["kind"] == "ins":
                        c, kp = u["args"]
                        m = 2 * c + kp
                        eng.wait_ge(dve_took, u["order"])
                        if c >= 1 and kp == 0:
                            eng.wait_ge(filled, pairs_of(b, stage, "out")[TPC * c - 1]["k"] + 1)
                        eng.activation(h_hi[:, 2 * kp:2 * kp + 2, :], hf[:, m % 2, :, :], ACT.Copy
                                       ).then_inc(hi_ready, 1)
                    if u["kind"] == "out":
                        t = u["args"][0]
                        eng.wait_ge(filled, u["k"] + 1)
                        if t >= 2:
                            eng.wait_ge(*took_at(pairs_of(b, stage, "out")[t - 2]))
                        eng.activation(osb[:, t % 2, :], pair[u["slot"]][:, 1, :], ACT.Copy).then_inc(os_ready, 1)

            for b in range(B):
                turn_in(LN * b)
                for u in stages[b, "attn_a"]:
                    h, c, i = u["args"]
                    m = b * HA * NC + h * NC + c
                    eng.wait_ge(filled, u["k"] + 1)
                    if m % (HA * NC) >= 2 and i == 0:
                        eng.wait_ge(av_done, m - 1)
                    if i + 1 < TPC * c:
                        eng.activation(aw[:, m % 2, i:i + 2, :], pair[u["slot"]][:, :, :], ACT.Sigmoid
                                       ).then_inc(act_took, 1)
                    else:
                        w0, w1 = diag_widths(c, i), diag_widths(c, i + 1)
                        eng.activation(aw[:, m % 2, i, w0:CH], pair[u["slot"]][:, 0, w0:CH], ACT.Sigmoid)
                        eng.activation(aw[:, m % 2, i + 1, w1:CH], pair[u["slot"]][:, 1, w1:CH], ACT.Sigmoid
                                       ).then_inc(act_took, 1)
                turn_in(LN * b + 1)
                ffn(b, "ffn0", 2 * b)
                turn_in(LN * b + 2)
                for u in stages[b, "qkv"]:
                    if u["kind"] == "q":
                        c, kp = u["args"]
                        eng.wait_ge(filled, u["k"] + 1)
                        eng.activation(qT_hi[:, 2 * kp:2 * kp + 2, c * CH:(c + 1) * CH], pair[u["slot"]][:, :, :],
                                       ACT.Copy).then_inc(qT_split, 1)
                    if u["kind"] == "k":
                        eng.wait_ge(filled, u["k"] + 1)
                        eng.activation(keys, pair[u["slot"]][:, :, :].rearrange("p a b -> p (a b)"), ACT.Copy,
                                       scale=float(DH) ** -0.5).then_inc(act_took, 1)
                    if u["kind"] == "v":
                        eng.wait_ge(filled, u["k"] + 1)
                        eng.activation(vb[:, :, 0:DH],
                                       pair[u["slot"]][:, 0, 0:NT * DH].rearrange("p (t d) -> p t d", d=DH),
                                       ACT.Copy).then_inc(act_took, 1)
                for n, u in enumerate(exp_list[b]):
                    eng.wait_ge(filled, u["k"] + 1)
                    if n == NPB - 1:
                        eng.wait_ge(kst_ready, (b + 1) * NT)
                    if n >= NPB:
                        qt, half, kt, _ = exp_list[b][n - NPB]["args"]
                        eng.wait_ge(pv_done, pv_index(b, qt, half, kt) + 1)
                    eng.activation(pb[:, n % NPB, :, :], pair[u["slot"]][:, :, :], ACT.Exp).then_inc(act_took, 1)
                turn_in(LN * b + 3)
                ffn(b, "ffn1", 2 * b + 1)

        @block.tensor
        def _(eng):
            def room(u):
                if u["k"] >= NPAIR:
                    eng.wait_ge(*took_at(units[u["k"] - NPAIR]))

            def turn(n):
                for t in range(NT):
                    eng.wait_ge(xn_ready, n * NT + t + 1)
                    if t >= 2:
                        eng.wait_ge(xnT_ready, n * NT + t - 1)
                    for kt in range(KT):
                        mm = eng.transpose(aux[t % 2][:, kt * P:(kt + 1) * P], xn[:, t, kt * P:(kt + 1) * P],
                                           ident[:, :])
                    mm.then_inc(xn_turned, 1)

            def ffn(b, stage, f):
                n = LN * b + (1 if stage == "ffn0" else 3)
                for u in stages[b, stage]:
                    room(u)
                    bank = pair[u["slot"]]
                    if u["kind"] == "logits":
                        for t in range(NT):
                            eng.wait_ge(xnT_ready, n * NT + t + 1)
                            for kt in range(KT):
                                mm = eng.matmul(bank[:, 0, t * E:(t + 1) * E], xnT[:, kt, t * P:(t + 1) * P],
                                                gateT[:, kt, :], start=(kt == 0), stop=(kt == KT - 1))
                    elif u["kind"] == "rT":
                        eng.wait_ge(soft_step, 6 * f + 6)
                        for t in range(NT):
                            mm = eng.transpose(bank[0:RS, t // TPC, t % TPC * P:(t % TPC + 1) * P], rstk[:, t, :],
                                               ident[:, :])
                    elif u["kind"] == "ins":
                        c, kp = u["args"]
                        eng.wait_ge(*took_at(pairs_of(b, stage, "rT")[0]))
                        for i in range(2):
                            k = 2 * kp + i
                            mm = eng.matmul(bank[:, i, :], scales[:, 0, k * P:(k + 1) * P], rT[:, c * CH:(c + 1) * CH],
                                            start=True, stop=True)
                    else:
                        t = u["args"][0]
                        c = t // TPC
                        eng.wait_ge(lo_ready, f * FFN_IN + 2 * c + 2)
                        eng.matmul(bank[:, 1, :], rT[:, t * P:(t + 1) * P], scales[:, 1, :], start=True, stop=True)
                        parts = [(h, kt) for h in (h_hi, h_lo) for kt in range(KT)]
                        for m, (h, kt) in enumerate(parts):
                            mm = eng.matmul(bank[:, 0, :], h[:, kt, t % TPC * P:(t % TPC + 1) * P], wT[:, kt, :],
                                            start=(m == 0), stop=(m == len(parts) - 1))
                    mm.then_inc(filled, 1)

            eng.wait_ge(const_ready, 11)
            eng.wait_ge(bind_step, 7)
            eng.transpose(aux[0][:, 0:HA], qks[:, :], ident[0:HA, 0:HA]).then_inc(setup_pe, 1)
            for h in range(HA):
                mm = eng.matmul(aux[1][:, h * P:(h + 1) * P], sel[:, h, :], bnd[:, 2, :], start=True, stop=True)
            mm.then_inc(setup_pe, 1)
            eng.wait_ge(small_loaded, 32)
            eng.matmul(pair[0][:, 0, :], ones1[:, :], bias1[:, :], start=True, stop=True).then_inc(setup_pe, 1)
            for kt in range(KT):
                mm = eng.transpose(pair[0][:, 1, kt * E:(kt + 1) * E], gate[:, kt * P:(kt + 1) * P], ident[0:E, 0:E])
            mm.then_inc(setup_pe, 1)
            eng.wait_ge(sign_ready, 1)
            for kt in range(KT):
                for o in range(KT):
                    mm = eng.transpose(pair[1 + kt // 2][:, kt % 2, o * P:(o + 1) * P], wsg[:, o, kt * P:(kt + 1) * P],
                                       ident[:, :])
                mm.then_inc(setup_pe, 1)
            eng.wait_ge(setup_out, 4 + KT)

            for b in range(B):
                turn(LN * b)
                us = stages[b, "attn_a"]

                def weigh(m):
                    h, c = divmod(m, NC)
                    n = b * HA * NC + m
                    last = [u for u in us if u["args"][:2] == (h, c)][-1]
                    eng.wait_ge(act_took, last["order"])
                    eng.wait_ge(aw_masked, TPC * (n + 1))
                    eng.wait_ge(va_ready, NT * (b + 1))
                    if n % (HA * NC) >= 2:
                        eng.wait_ge(xa_added, n - 1)
                    for t in range(TPC * c, TPC * c + TPC):
                        lo = (t - TPC * c) * P
                        for i in range(t + 1):
                            mm = eng.matmul(aux[n % 2][:, lo:lo + P], aw[:, n % 2, i, lo:lo + P],
                                            va[:, i, h * P:(h + 1) * P], start=(i == 0), stop=(i == t))
                    mm.then_inc(av_done, 1)

                eng.wait_ge(xnT_ready, (LN * b + 1) * NT)
                for u in us:
                    h, c, i0 = u["args"]
                    m = h * NC + c
                    room(u)
                    eng.wait_ge(qT_ready, b * HA + h + 1)
                    for i in (i0, i0 + 1):
                        w = diag_widths(c, i)
                        mm = eng.matmul(pair[u["slot"]][:, i - i0, w:CH], xnT[:, h, i * P:(i + 1) * P],
                                        qT[:, h, c * CH + w:(c + 1) * CH], start=True, stop=True)
                    mm.then_inc(filled, 1)
                    if i0 + 2 == TPC * (c + 1) and m >= 1:
                        weigh(m - 1)
                weigh(HA * NC - 1)

                turn(LN * b + 1)
                ffn(b, "ffn0", 2 * b)

                turn(LN * b + 2)
                eng.wait_ge(xnT_ready, (LN * b + 3) * NT)
                eng.wait_ge(pads_ready, 11)
                eng.wait_ge(halves_zeroed, 2)
                for u in stages[b, "qkv"]:
                    room(u)
                    bank = pair[u["slot"]]
                    if u["kind"] == "v":
                        for t in range(NT):
                            for kt in range(KT):
                                mm = eng.matmul(bank[:, 0, t * DH:(t + 1) * DH], xnT[:, kt, t * P:(t + 1) * P],
                                                wqkv[:, kt, HB * DH + DH:HB * DH + 2 * DH],
                                                start=(kt == 0), stop=(kt == KT - 1))
                    elif u["kind"] == "k":
                        for c in range(NC):
                            for kt in range(KT):
                                mm = eng.matmul(bank[:, c, :], wk[:, kt, :, :].rearrange("p j d -> p (j d)"),
                                                xnT[:, kt, c * CH:(c + 1) * CH],
                                                start=(kt == 0), stop=(kt == KT - 1))
                    else:
                        c, kp = u["args"]
                        for i in range(2):
                            m = (2 * kp + i) * P
                            for kt in range(KT):
                                mm = eng.matmul(bank[:, i, :], wqkv[:, kt, m:m + P], xnT[:, kt, c * CH:(c + 1) * CH],
                                                start=(kt == 0), stop=(kt == KT - 1))
                    mm.then_inc(filled, 1)

                eng.wait_ge(*took_at(pairs_of(b, "qkv", "q")[-1]))
                eng.wait_ge(*took_at(pairs_of(b, "qkv", "v")[-1]))
                for e in stages[b, "attn_b"]:
                    if e[0] == "pv":
                        _, qt, half, kt = e
                        n = pv_index(b, qt, half, kt)
                        if kt == 0 and qt * 2 + half >= 2:
                            eng.wait_ge(ot_ready, (b * NT + qt) * 2 + half - 1)
                        for gp in range(2):
                            u = exp_units[b, qt, half, kt, gp]
                            eng.wait_ge(act_took, u["order"])
                            for i in range(2):
                                j = 2 * gp + i
                                mm = eng.matmul(aux[half][j * QR:(j + 1) * QR, :], vb[:, kt, :],
                                                pb[:, exp_list[b].index(u) % NPB, i, :], start=(kt == 0), stop=(kt == qt),
                                                tile_position=(0, j * QR))
                        mm.then_inc(pv_done, 1)
                        continue
                    u = e[1]
                    bank = pair[u["slot"]]
                    room(u)
                    if u["kind"] == "max":
                        qt, c, g = u["args"]
                        w = min(CH, (qt + 1) * P - c * CH)
                        diag = c == qt // TPC
                        eng.wait_ge(kst_ready, b * NT + 2 * (qt // 2) + 2)
                        eng.wait_ge(stack_moved[qt // 2], 16 * 28 * (b + 1))
                        for i in range(2):
                            mm = eng.matmul(bank[:, i, 0:w],
                                            qs[:, qt // 2 % NQS, g, qt % 2 * P:(qt % 2 + 1) * P],
                                            kst[qt // 2][:, i, c * CH:c * CH + w], start=True, stop=not diag)
                        if diag:
                            for i in range(2):
                                mm = eng.matmul(bank[:, i, w - P:w], identb[:, :], negtri[:, :], start=False, stop=True)
                    elif u["kind"] == "mt":
                        qt = u["args"][0]
                        if qt < TPC:
                            eng.wait_ge(*took_at(max_last[b, qt]))
                        else:
                            eng.wait_ge(max_ready, b * (NT - TPC) + qt - TPC + 1)
                        mm = eng.transpose(bank[0:HB, 0, 0:P], nmx[:, qt % 2, :], ident[:, :])
                    elif u["kind"] == "exp":
                        qt, half, kt, gp = u["args"]
                        g = (2 * half + gp) * GQ
                        eng.wait_ge(max_moved[qt % 2], 16 * 4 * ((b * NT + qt) // 2 + 1))
                        for i in range(2):
                            mm = eng.matmul(bank[:, i, :], kst[qt // 2][:, i, kt * P:(kt + 1) * P],
                                            qs[:, qt // 2 % NQS, g:g + GQ, qt % 2 * P:(qt % 2 + 1) * P],
                                            start=True, stop=kt < qt)
                        if kt == qt:
                            for i in range(2):
                                mm = eng.matmul(bank[:, i, :], identb[:, :],
                                                negtriT[:, :].unsqueeze(1).to_broadcast([P, GQ, P]),
                                                start=False, stop=True)
                    elif u["kind"] == "ot":
                        qt, half = u["args"]
                        eng.wait_ge(ot_ready, (b * NT + qt) * 2 + half + 1)
                        for g in range(GQ):
                            mm = eng.transpose(bank[:, 0, g * P:(g + 1) * P], otS[:, half, g * P:(g + 1) * P], ident[:, :])
                    elif u["kind"] == "tt":
                        qt = u["args"][0]
                        eng.wait_ge(*took_at(ot_units[b, qt, 1]))
                        for kt in range(KT):
                            mm = eng.transpose(bank[:, 0, kt * P:(kt + 1) * P], att[:, qt % 2, kt * P:(kt + 1) * P],
                                               ident[:, :])
                    else:
                        qt = u["args"][0]
                        eng.wait_ge(*took_at(tt_units[b, qt]))
                        for kt in range(KT):
                            mm = eng.matmul(bank[:, 0, :], attT[:, qt % 2, kt * P:(kt + 1) * P], wo[:, kt, :],
                                            start=(kt == 0), stop=(kt == KT - 1))
                    mm.then_inc(filled, 1)

                turn(LN * b + 3)
                ffn(b, "ffn1", 2 * b + 1)

        @block.vector
        def _(eng):
            eng.memset(kst_all[HP:P, 0, :].bitcast(F32), 0.0).then_inc(halves_zeroed, 1)
            eng.memset(kst_all[0:HP, 1, :].bitcast(F32), 0.0).then_inc(halves_zeroed, 1)
            eng.wait_ge(bind_loaded, 48)
            eng.tensor_reduce(alpha[:, :], bv[:, :, :], AX.X, ALU.add, apply_absolute_value=True).then_inc(bind_step, 1)
            eng.tensor_scalar(bsg[:, :, :], bv[:, :, :], 0.0, 2.0, ALU.is_ge, ALU.mult).then_inc(bind_step, 1)
            eng.wait_ge(bind_step, 2)
            eng.tensor_scalar(alpham[:, :], alpha[:, :], 1.0 / P, None, ALU.mult).then_inc(bind_step, 1)
            eng.wait_ge(bind_step, 3)
            eng.scalar_tensor_tensor(out=hard[:, :, :], in0=bsg[:, :, :], scalar=-1.0,
                                     in1=alpham[:, :].unsqueeze(2).to_broadcast([HA, 3, P]),
                                     op0=ALU.add, op1=ALU.mult).then_inc(bind_step, 1)
            eng.wait_ge(bind_step, 4)
            eng.tensor_tensor(bdf[:, :, :], hard[:, :, :], bv[:, :, :], ALU.subtract).then_inc(bind_step, 1)
            eng.wait_ge(bind_step, 5)
            eng.tensor_tensor(bnd[:, :, :], bdf[:, :, :], bv[:, :, :], ALU.add).then_inc(bind_step, 1)
            eng.wait_ge(bind_step, 6)
            eng.scalar_tensor_tensor(out=qks[:, :], in0=bnd[:, 0, :], scalar=4.0 * float(P) ** -0.5,
                                     in1=bnd[:, 1, :], op0=ALU.mult, op1=ALU.mult).then_inc(bind_step, 1)
            eng.wait_ge(setup_pe, 1)
            eng.tensor_copy(wqk[:, :], aux[0][:, 0:HA]).then_inc(setup_out, 1)
            eng.wait_ge(setup_pe, 2)
            eng.tensor_copy(vbc[:, :], aux[1][:, :]).then_inc(setup_out, 1)
            eng.wait_ge(setup_pe, 4)
            eng.tensor_copy(bias_bc[:, :], pair[0][:, 0, :]).then_inc(setup_out, 1)
            eng.tensor_copy(gateT[:, :, :], pair[0][:, 1, 0:KT * E].rearrange("p (k e) -> p k e", e=E)
                            ).then_inc(setup_out, 1)
            for kt in range(KT):
                eng.wait_ge(setup_pe, 5 + kt)
                eng.tensor_copy(wT[:, kt, :], pair[1 + kt // 2][:, kt % 2, :]).then_inc(setup_out, 1)

            eng.wait_ge(scales_loaded, 128)
            eng.tensor_copy(scales[:, :, :], scale_raw).then_inc(scales_step, 1)
            eng.wait_ge(cq_loaded, 16)
            eng.tensor_copy(cq[:, :, :], cq_raw).then_inc(cq_ready, 1)
            eng.wait_ge(scales_step, 1)
            eng.tensor_tensor(scale_lo[QR:RS], scale_raw[QR:RS], scales[QR:RS, :, :].bitcast(F32), ALU.subtract
                              ).then_inc(scales_step, 1)
            eng.wait_ge(scales_step, 2)
            eng.tensor_copy(scales[QR:RS, :, :], scale_lo[QR:RS]).then_inc(scales_step, 1)

            def norm(n, ready):
                for t in range(NT):
                    ready(t)
                    eng.bn_stats(st[:, t, :], x[:, t, :]).then_inc(ln_stats, 1)
                for t in range(NT):
                    eng.wait_ge(ln_stats, n * NT + t + 1)
                    eng.bn_aggr(mv[:, t, :], st[:, t, :]).then_inc(ln_aggr, 1)
                eng.wait_ge(ln_aggr, (n + 1) * NT)
                eng.tensor_scalar(ve[:, :], mv[:, :, 1], EPS, None, ALU.add).then_inc(ln_var, 1)
                eng.wait_ge(ln_rstd, n + 1)
                for t in range(NT):
                    eng.tensor_scalar(xn[:, t, :], x[:, t, :], mv[:, t, 0:1], rstd[:, t:t + 1],
                                      ALU.subtract, ALU.mult).then_inc(xn_ready, 1)

            def ffn(b, stage, f):
                for u in stages[b, stage]:
                    bank = pair[u["slot"]]
                    if u["kind"] == "logits":
                        lg = bank[:, 0, 0:NT * E].rearrange("p (t e) -> p t e", e=E)
                        eng.wait_ge(filled, u["k"] + 1)
                        eng.tensor_reduce(lmax[:, :], lg, AX.X, ALU.max).then_inc(soft_step, 1)
                        eng.wait_ge(soft_step, 6 * f + 1)
                        eng.tensor_tensor(lsub[:, :, :], lg, lmax[:, :].unsqueeze(2).to_broadcast([P, NT, E]),
                                          ALU.subtract).then_inc(soft_step, 1)
                        eng.wait_ge(soft_step, 6 * f + 2)
                        eng.wait_ge(exp_ready, f + 1)
                        eng.tensor_reduce(lsum[:, :], lexp[:, :, :], AX.X, ALU.add).then_inc(dve_took, 1)
                        eng.wait_ge(dve_took, u["order"])
                        eng.reciprocal(lrec[:, :], lsum[:, :]).then_inc(soft_step, 1)
                        eng.wait_ge(soft_step, 6 * f + 3)
                        eng.tensor_tensor(rt[:, :, :], lexp[:, :, :], lrec[:, :].unsqueeze(2).to_broadcast([P, NT, E]),
                                          ALU.mult).then_inc(soft_step, 1)
                        eng.wait_ge(soft_step, 6 * f + 4)
                        eng.tensor_copy(rt_hi[:, :, :], rt[:, :, :]).then_inc(rt_split, 1)
                        eng.wait_ge(rt_split, f + 1)
                        places = rstk[:, :, :].rearrange("p t (a e) -> p t a e", a=2)
                        both = [P, NT, 2, E]
                        hi = rt_hi[:, :, :].bitcast(F32).unsqueeze(2).to_broadcast(both)
                        eng.tensor_copy(places[:, :, :, 0:E], hi).then_inc(soft_step, 1)
                        eng.tensor_tensor(places[:, :, :, E:2 * E], rt[:, :, :].unsqueeze(2).to_broadcast(both), hi,
                                          ALU.subtract).then_inc(soft_step, 1)
                    if u["kind"] == "ins":
                        c, kp = u["args"]
                        m = 2 * c + kp
                        eng.wait_ge(filled, u["k"] + 1)
                        if m >= 2:
                            eng.wait_ge(hi_ready, f * FFN_IN + m - 1)
                            eng.wait_ge(lo_ready, f * FFN_IN + m - 1)
                        eng.tensor_tensor(hf[:, m % 2, :, :], bank[:, :, :],
                                          xnT[:, 2 * kp:2 * kp + 2, c * CH:(c + 1) * CH], ALU.mult
                                          ).then_inc(dve_took, 1)
                        eng.wait_ge(hi_ready, f * FFN_IN + m + 1)
                        eng.tensor_tensor(h_lo[:, 2 * kp:2 * kp + 2, :], hf[:, m % 2, :, :],
                                          h_hi[:, 2 * kp:2 * kp + 2, :].bitcast(F32), ALU.subtract
                                          ).then_inc(lo_ready, 1)
                    if u["kind"] == "out":
                        t = u["args"][0]
                        n = f * NT + t
                        eng.wait_ge(os_ready, n + 1)
                        eng.tensor_tensor(tmp[:, t % 2, :], bank[:, 0, :], osb[:, t % 2, :], ALU.mult
                                          ).then_inc(dve_took, 1)
                        eng.wait_ge(dve_took, u["order"])
                        eng.wait_ge(biased, n + 1)
                        eng.tensor_tensor(x[:, t, :], tmp[:, t % 2, :], x[:, t, :], ALU.add).then_inc(xf_added, 1)

            for b in range(B):
                norm(LN * b, lambda t: eng.wait_ge(x_loaded[t // 2], 16 * (b + 1)))
                for h in range(HA):
                    eng.wait_ge(xnT_ready, (LN * b + 1) * NT)
                    eng.tensor_scalar(qT[:, h, :], xnT[:, h, :], wqk[:, h:h + 1], None, ALU.mult).then_inc(qT_ready, 1)
                for m in range(HA * NC):
                    h, c = divmod(m, NC)
                    n = b * HA * NC + m
                    xs = x[:, TPC * c:TPC * c + TPC, h * P:(h + 1) * P]
                    eng.wait_ge(av_done, n + 1)
                    eng.tensor_tensor(xs, aux[n % 2][:, :].rearrange("p (t q) -> p t q", q=P), xs, ALU.add
                                      ).then_inc(xa_added, 1)
                norm(LN * b + 1, lambda t: eng.wait_ge(xa_added, (b + 1) * HA * NC))
                ffn(b, "ffn0", 2 * b)
                norm(LN * b + 2, lambda t: eng.wait_ge(xf_added, 2 * b * NT + t + 1))
                for u in stages[b, "qkv"]:
                    if u["kind"] == "q":
                        c, kp = u["args"]
                        eng.wait_ge(qT_split, 4 * b + 2 * c + kp + 1)
                        eng.tensor_tensor(qT_lo[:, 2 * kp:2 * kp + 2, c * CH:(c + 1) * CH], pair[u["slot"]][:, :, :],
                                          qT_hi[:, 2 * kp:2 * kp + 2, c * CH:(c + 1) * CH].bitcast(F32), ALU.subtract
                                          ).then_inc(dve_took, 1)
                    if u["kind"] == "k":
                        eng.wait_ge(*took_at(u))
                        for n, r in enumerate((QR, HP + QR)):
                            eng.tensor_copy(kst[-1][r:r + DH, n, :], keys[r:r + DH, :]).then_inc(keys_step, 1)
                            eng.wait_ge(keys_step, 4 * b + 2 * n + 1)
                            eng.tensor_tensor(keys[r:r + DH, :], keys[r:r + DH, :], kst[-1][r:r + DH, n, :].bitcast(F32),
                                              ALU.subtract).then_inc(keys_step, 1)
                for e in stages[b, "attn_b"]:
                    if e[0] == "pv":
                        _, qt, half, kt = e
                        if kt == qt:
                            n = (b * NT + qt) * 2 + half
                            eng.wait_ge(pv_done, pv_index(b, qt, half, kt) + 1)
                            if qt > 0:
                                eng.wait_ge(filled, ot_units[b, qt - 1, half]["k"] + 1)
                            eng.tensor_copy(otS[:, half, :], aux[half][:, :]).then_inc(ot_ready, 1)
                        continue
                    u = e[1]
                    bank = pair[u["slot"]]
                    if u["kind"] == "exp":
                        continue
                    eng.wait_ge(filled, u["k"] + 1)
                    if u["kind"] == "max":
                        qt, c, g = u["args"]
                        w = min(CH, (qt + 1) * P - c * CH)
                        o = mx[:, qt % 2, c, :] if qt >= TPC else nmx[:, qt % 2, :]
                        if qt < TPC and qt >= 2 and g == 0:
                            eng.wait_ge(filled, mt_units[b, qt - 2]["k"] + 1)
                        o = o.rearrange("p (j g) -> p j g", j=2)[:, :, g]
                        ins = eng.tensor_reduce(o, bank[:, :, 0:w], AX.X, ALU.max, negate=True)
                        ins.then_inc(dve_took, 1)
                        if c == qt // TPC and g == G - 1:
                            eng.wait_ge(dve_took, u["order"])
                            if qt >= TPC:
                                eng.wait_ge(filled, mt_units[b, qt - 2]["k"] + 1)
                                eng.tensor_tensor(nmx[:, qt % 2, :], mx[:, qt % 2, 0, :], mx[:, qt % 2, 1, :], ALU.min
                                                  ).then_inc(max_ready, 1)
                    elif u["kind"] == "mt":
                        qt = u["args"][0]
                        if qt >= 2:
                            eng.wait_ge(max_moved[qt % 2], 16 * 4 * ((b * NT + qt) // 2))
                        eng.tensor_copy(mT_hi[:, qt % 2, :], bank[0:HB, 0, 0:P]).then_inc(max_split, 1)
                        eng.wait_ge(max_split, b * NT + qt + 1)
                        eng.tensor_tensor(mT_lo[:, qt % 2, :], bank[0:HB, 0, 0:P], mT_hi[:, qt % 2, :].bitcast(F32),
                                          ALU.subtract).then_inc(dve_took, 1)
                    elif u["kind"] == "ot":
                        qt, half = u["args"]
                        o = bank[:, 0, :].rearrange("p (h d) -> p h d", d=QR)
                        eng.reciprocal(rec[:, half, :].unsqueeze(2), o[:, :, DH:DH + 1]).then_inc(rec_ready, 1)
                        eng.wait_ge(rec_ready, (b * NT + qt) * 2 + half + 1)
                        eng.tensor_tensor(att[:, qt % 2, half * HB // 2 * DH:(half + 1) * HB // 2 * DH]
                                          .rearrange("p (h d) -> p h d", d=DH), o[:, :, 0:DH],
                                          rec[:, half, :].unsqueeze(2).to_broadcast([P, HB // 2, DH]), ALU.mult
                                          ).then_inc(dve_took, 1)
                    elif u["kind"] == "tt":
                        qt = u["args"][0]
                        eng.tensor_copy(attT[:, qt % 2, :], bank[:, 0, :]).then_inc(dve_took, 1)
                    elif u["kind"] == "wo":
                        qt = u["args"][0]
                        eng.tensor_tensor(x[:, qt, :], bank[:, 0, :], x[:, qt, :], ALU.add).then_inc(dve_took, 1)
                norm(LN * b + 3, lambda t: eng.wait_ge(*took_at(wo_units[b, t])))
                ffn(b, "ffn1", 2 * b + 1)


def split12(v):
    hi = (((v.view(np.uint32) + np.uint32(0x800)) >> np.uint32(12)) << np.uint32(12)).view(np.float32)
    return hi, v - hi


def constants():
    base = 2.0 ** (-2.0 ** (-(np.log2(HB) - 3)))
    slope = (base ** np.arange(1, HB + 1, dtype=np.float64)).astype(np.float32)
    cq = np.zeros((2, 2, NFIX, G, P), np.float32)
    ramp = np.zeros((P, T), np.float32)
    for j in range(2):
        for g in range(G):
            half, gp, g4 = g // 8, g // 4 % 2, g % 4
            s = slope[16 * half + 4 * g4 + 2 * gp + j]
            for a in range(2):
                cq[a, j, 0, g, :], cq[a, j, 1, g, :] = split12(np.full(P, s, np.float32))
                off = (-s.astype(np.float64) * (a * P + np.arange(P))).astype(np.float32)
                cq[a, j, 2, g, :], cq[a, j, 3, g, :] = split12(off)
        ramp[j * HP + R_SLOPE:j * HP + R_OFF, :] = np.arange(T) - (T - 2 * P)
        ramp[j * HP + R_OFF:j * HP + R_MAX + 2, :] = 1.0
    cq = cq.reshape(4 * NFIX, G, P)
    return cq, ramp


_INS = ["L0_attn_a_x", "L0_attn_a_bv_q", "L0_attn_a_bv_k", "L0_attn_a_bv_v", "L0_attn_b_Wqkv", "L0_attn_b_Wo",
        "L0_ffn_weight", "L0_ffn_bias", "L0_ffn_gate_w", "L0_ffn_in_channel_scale", "L0_ffn_out_channel_scale"]


def kernel(**inputs):
    import concourse.bacc as _bacc
    from concourse.bass_utils import run_bass_kernel_spmd as _run

    nc = _bacc.Bacc("TRN2", target_bir_lowering=False, num_devices=1)
    arrays = {f"in_{n}_dram": np.ascontiguousarray(inputs[n]) for n in _INS}
    cq, ramp = constants()
    arrays["slope_rows_dram"], arrays["position_rows_dram"] = cq, ramp
    args = [nc.dram_tensor(n, a.shape, mybir.dt.from_np(a.dtype), kind="ExternalInput").ap() for n, a in arrays.items()]
    out = nc.dram_tensor("out_0_dram", (B, T, D), F32, kind="ExternalOutput").ap()
    build(nc, *args, out)
    r = _run(nc, [arrays], core_ids=[0])
    return r.results[0]["out_0_dram"]
```

```python
from contextlib import ExitStack

import numpy as np

import concourse.bass as bass
import concourse.mybir as mybir

F32 = mybir.dt.float32
F32R = mybir.dt.float32r
BF16 = mybir.dt.bfloat16
ALU = mybir.AluOpType
ACT = mybir.ActivationFunctionType
AX = mybir.AxisListType

B, T, D = 2, 1024, 512
P = 128
NT = T // P
KT = D // P
CH = 512
NC = T // CH
TPC = CH // P
HA = 4
HB, DH = 32, 16
HP = P // 2
G = HB // 2
GQ = 4
QR = 32
E = 8
EPS = 1e-5
NEG = -1e30
R_SLOPE, R_OFF, R_MAX = 3 * DH, 3 * DH + 2, 3 * DH + 4
R_VALUE = R_SLOPE
NFIX = HP - R_SLOPE
NQS = 3
RS = 64
NPAIR = 3
NPB = 6
WORK = 2 * HA * T + 4 * TPC * CH + KT * CH
NKST = sum(2 * P * (a + 1) for a in range(NT // 2))
LEAD = 4
MAX_RATE = 3
THIRD_BEHIND = 1
MOVE_BEHIND = 4
TAIL_AT = 52
KEYS_AT = 3
GROUP_ORDER = ("exp", "max", "pv", "exp", "max")
LAG = 2


def plan():
    units, events, count = [], [], {"act": 0, "dve": 0}

    def unit(who, kind, *args):
        count[who] += 1
        units.append(dict(kind=kind, args=args, who=who, order=count[who], k=len(units), slot=len(units) % NPAIR))
        events.append(("unit", units[-1]))

    def step(kind, *args):
        events.append((kind,) + args)

    def norm(b, l, c, stats=TPC):
        for t in range(TPC * (c + 1) - stats, TPC * (c + 1)):
            step("stats", b, l, t)
        step("norm", b, l, c)

    def turn(b, l, c):
        for t in range(TPC * c, TPC * (c + 1), 2):
            unit("act", "turn", b, l, t)

    def outs(b, f, *tiles):
        for t in tiles:
            unit("dve", "out", b, f, t)
            if f == 1 and t % 2 == 1:
                step("store", b, t - 1)

    def head(b):
        norm(b, 0, 0)
        turn(b, 0, 0)
        step("qT", b, 0)

    def sigs(b, m):
        for i in range(0, TPC * (m // HA + 1), 2):
            unit("act", "sig", b, m, i)

    def attn_a(b, first, last, *between):
        between = list(between)
        for m in range(first, last):
            c = m // HA
            for i in range(0, TPC * (c + 1), 2):
                unit("act", "sig", b, m, i)
                if between:
                    between.pop(0)()
            if m >= 1:
                step("weigh", b, m - 1)

    head(0)
    step("va", 0, 0)
    attn_a(0, 0, 1)
    norm(0, 0, 1)
    step("va", 0, 1)
    attn_a(0, 1, 2)
    unit("dve", "small", 0)
    step("channel_scales")
    step("sign")
    for b in range(B):
        if b == 0:
            attn_a(b, 2, 3)
            attn_a(b, 3, HA)
        else:
            step("weigh", b, 2)
            norm(b, 0, 1)
            step("va", b, 1)
        turn(b, 0, 1)
        step("qT", b, 1)
        if b == 0:
            unit("dve", "wT", 0, 0)
            unit("dve", "wT", 0, 1)
            step("halves")
        attn_a(b, HA, HA + 1)
        norm(b, 1, 0)
        attn_a(b, HA + 1, HA + 2)
        turn(b, 1, 0)
        unit("dve", "logits", b, 0, 0)
        attn_a(b, HA + 2, HA + 3, lambda: step("soft", b, 0, 0), lambda: unit("act", "rT", b, 0, 0),
               lambda: unit("dve", "ins", b, 0, 0, 0), lambda: unit("dve", "ins", b, 0, 0, 1))
        attn_a(b, HA + 3, NC * HA, *[lambda t=t: outs(b, 0, t) for t in range(TPC)])
        norm(b, 2, 0)
        step("weigh", b, NC * HA - 1)
        norm(b, 1, 1)
        turn(b, 2, 0)
        unit("dve", "q", b, 0, 0)
        turn(b, 1, 1)
        unit("dve", "logits", b, 0, 1)
        unit("dve", "q", b, 0, 1)
        step("soft", b, 0, 1)
        unit("act", "rT", b, 0, 1)
        unit("dve", "ins", b, 0, 1, 0)
        unit("dve", "ins", b, 0, 1, 1)
        unit("dve", "q", b, 0, 2)
        unit("dve", "q", b, 0, 3)
        step("stack", b, 0)
        step("stack", b, 1)
        outs(b, 0, *range(TPC, NT))
        norm(b, 2, 1)
        unit("act", "k", b, 0)
        unit("act", "v", b, 0)
        first, rest = softmax_events()

        def softmax(e):
            if e[0] == "unit":
                unit("act" if e[1] in ("exp", "tt") else "dve", e[1], b, *e[2:])
                if e[1] == "mt" and e[2] == THIRD_BEHIND:
                    step("stack", b, 2)
                if e[1] == "mt" and e[2] == MOVE_BEHIND:
                    step("stack", b, 3)
            else:
                step(e[0], b, *e[1:])

        turn(b, 2, 1)
        for k in range(KT):
            unit("dve", "q", b, 1, k)
        unit("act", "k", b, 1)
        unit("act", "v", b, 1)
        for e in first:
            softmax(e)
        tail = [lambda: norm(b, 3, 0), lambda: turn(b, 3, 0), lambda: unit("dve", "logits", b, 1, 0),
                lambda: step("soft", b, 1, 0), lambda: step("stats", b, 3, TPC),
                lambda: unit("act", "rT", b, 1, 0),
                lambda: unit("dve", "ins", b, 1, 0, 0), lambda: unit("dve", "ins", b, 1, 0, 1),
                lambda: outs(b, 1, 0), lambda: outs(b, 1, 1),
                lambda: step("stats", b, 3, TPC + 1), lambda: outs(b, 1, 2), lambda: outs(b, 1, 3)]
        if b + 1 < B:
            tail += [lambda: None, lambda: norm(b + 1, 0, 0), lambda: None,
                     lambda: turn(b + 1, 0, 0), lambda: step("qT", b + 1, 0)]
        group = 0
        for e in rest:
            softmax(e)
            if e[0] == "pv":
                group += 1
                if group > TAIL_AT and tail:
                    tail.pop(0)()
            if e == ("unit", "ot", NT - 1, 1) and b + 1 < B:
                assert not tail
                step("va", b + 1, 0)
                attn_a(b + 1, 0, 1)
        assert not tail
        norm(b, 3, 1, TPC - 2)
        if b + 1 < B:
            attn_a(b + 1, 1, 2)
        turn(b, 3, 1)
        unit("dve", "logits", b, 1, 1)
        step("soft", b, 1, 1)
        if b + 1 < B:
            sigs(b + 1, 2)
        unit("act", "rT", b, 1, 1)
        unit("dve", "ins", b, 1, 1, 0)
        unit("dve", "ins", b, 1, 1, 1)
        if b + 1 < B:
            step("weigh", b + 1, 1)
            sigs(b + 1, 3)
        outs(b, 1, *range(TPC, NT))
    return units, events


def softmax_events():
    groups = [(qt, half, kt) for qt in range(NT) for half in range(2) for kt in range(qt + 1)]
    extra = [[] for _ in groups]
    at, room_left = len(groups), 0
    first = []
    for qt in reversed(range(NT)):
        start = qt * (qt + 1) - LEAD
        if at > start:
            at, room_left = start, MAX_RATE
        us = [("mt", qt)] + [("max", qt, c, g) for c in reversed(range(qt // TPC + 1)) for g in reversed(range(G))]
        for u in us:
            if room_left == 0:
                at, room_left = at - 1, MAX_RATE
            (extra[at] if at >= 0 else first).insert(0, ("unit",) + u)
            if u[0] == "max":
                room_left -= 1
    ev = []
    waiting = []
    for n, (qt, half, kt) in enumerate(groups):
        ahead = extra[n]
        waiting.append((qt, half, kt))
        exps = [("unit", "exp", qt, half, kt, gp) for gp in range(2)]
        for what in GROUP_ORDER:
            if what == "exp":
                ev.append(exps.pop(0))
            elif what == "max" and ahead:
                ev.append(ahead.pop(0))
            elif what == "pv" and len(waiting) > LAG:
                q2, h2, k2 = waiting.pop(0)
                ev.append(("pv", q2, h2, k2))
                ev += after(q2, h2, k2)
        ev += ahead
    for q2, h2, k2 in waiting:
        ev.append(("pv", q2, h2, k2))
        ev += after(q2, h2, k2)
    return first, put_off(ev)


def after(qt, half, kt):
    if kt < qt:
        return []
    return [("late", 1, ("unit", "ot", qt, half))] + ([("late", 2, ("unit", "tt", qt)), ("late", 3, ("unit", "wo", qt))] if half == 1 else [])


def put_off(ev):
    out, late = [], []
    for e in ev:
        if e[0] == "late":
            late.append([e[1], e[2]])
            continue
        out.append(e)
        if e[0] == "pv":
            for x in late:
                x[0] -= 1
            out += [x[1] for x in late if x[0] <= 0]
            late = [x for x in late if x[0] > 0]
    return out + [x[1] for x in late]


def build(nc, x_in, bv_q, bv_k, bv_v, wqkv_in, wo_in, w_in, bias_in, gate_in, ics_in, ocs_in, cq_in, ramp_in, out):
    units, events = plan()

    with ExitStack() as ctx:
        def sb(name, shape, dt=F32):
            return ctx.enter_context(nc.sbuf_tensor(name, shape, dt))

        def psum(name, shape, dt=F32):
            return ctx.enter_context(nc.psum_tensor(name, shape, dt))

        def sem(name):
            return ctx.enter_context(nc.semaphore(name))

        x = sb("x", [P, NT, D])
        xnT = sb("xnT", [P, KT, T])
        h_split = sb("h_split", [P, 2, KT, CH], F32R)
        h_hi, h_lo = h_split[:, 0, :, :], h_split[:, 1, :, :]
        with nc.sbuf_tensor("xn", [P, NT, D], F32) as xn:
            pass
        qT_hi = sb("qT_hi", [P, NC, KT, CH], F32R)
        with nc.sbuf_tensor("work", [P, WORK], F32) as work:
            pass
        with nc.sbuf_tensor("before_early", [P, WORK - KT * CH], F32):
            with nc.sbuf_tensor("q_early", [P, KT, CH], F32R) as q_early:
                pass
        qT_lo = [q_early, h_lo]
        qs = sb("qs", [P, NQS, G, 2 * P], F32R)
        pb = sb("pb", [P, NPB, 2, CH])
        with nc.sbuf_tensor("signs", [P, 2, KT, D], F32) as signs:
            pass
        kst_all = sb("kst_all", [P, 2, NKST], F32R)
        qs_words = qs[:, :, :, :].bitcast(F32)
        wqkv = sb("wqkv", [P, KT, HB * DH + 2 * DH])
        wk = sb("wk", [P, KT, 2, HP])
        wo = sb("wo", [P, KT, D])
        wT = sb("wT", [P, KT, D], F32R)
        narrow = sb("narrow", [P, T + 2 * D], F32R)
        rT = narrow[0:RS, 0:T]
        scales = narrow[0:RS, T:T + 2 * D].rearrange("r (a n) -> r a n", a=2)
        gateT = sb("gateT", [P, KT, E])
        bias_bc = sb("bias_bc", [P, D])
        vbc = sb("vbc", [P, D])
        wqk = sb("wqk", [P, HA])
        cq = narrow[P - 4 * NFIX:P, :].rearrange("r (g q) -> r g q", q=P)
        ramp = sb("ramp", [P, T])
        alpha = sb("alpha", [HA, 3])
        alpham = sb("alpham", [HA, 3])
        ones1 = sb("ones1", [1, P])
        ident = sb("ident", [P, P])
        identb = sb("identb", [P, P], BF16)
        negtri = sb("negtri", [P, P], BF16)
        negtriT = sb("negtriT", [P, P], BF16)
        neghalf = sb("neghalf", [P, NT])
        key_scale = sb("key_scale", [P, 2])
        st = sb("st", [P, NT, 6])
        mv = sb("mv", [P, NT, 2])
        ve = sb("ve", [P, NT])
        rstd = sb("rstd", [P, NT])
        lmax = sb("lmax", [P, NT])
        lsub = sb("lsub", [P, NT, E])
        lexp = sb("lexp", [P, NT, E])
        lsum = sb("lsum", [P, NT])
        lrec = sb("lrec", [P, NT])
        rt = sb("rt", [P, NT, E])
        rt_hi = sb("rt_hi", [P, NT, E], F32R)
        rstk = sb("rstk", [P, NT, RS])
        vb = sb("vb", [P, NT, QR])
        mx = sb("mx", [P, 2, 2, HB])
        nmx = sb("nmx", [P, 2, HB])
        mT_hi = sb("mT_hi", [HB, 2, P], F32R)
        mT_lo = sb("mT_lo", [HB, 2, P], F32R)
        rec = sb("rec", [P, 2, HB // 2])

        NQS_WORDS = G * 2 * P
        assert NQS_WORDS == HA * T == 2 * TPC * CH

        def area(at, *shape):
            n = int(np.prod(shape))
            names = "abcd"[:len(shape)]
            v = work[:, at:at + n]
            if len(shape) > 1:
                v = v.rearrange(f"p ({' '.join(names)}) -> p {' '.join(names)}", **dict(zip(names[1:], shape[1:])))
            return v

        qT = area(NQS_WORDS, HA, T)
        aw = [area(2 * NQS_WORDS, 2 * TPC, CH), area(0, 2 * TPC, CH)]
        va = area(3 * NQS_WORDS, NT, D)
        in_xn = xn[:, TPC:2 * TPC, :].rearrange("p (a b) n -> p a b n", a=2)
        hf = [in_xn, area(2 * NQS_WORDS + TPC * CH, 2, 2, CH)]
        osb = [[xn[:, 0:2, :], area(2 * NQS_WORDS, 2, D)], [xn[:, 0:2, :], area(TPC * CH, 2, D)]]
        xnT_early = area(2 * HA * T + 4 * TPC * CH, KT, CH)
        wraw, wsg = signs[:, 0, :, :], signs[:, 1, :, :]
        at = 2 * NQS_WORDS
        bv, hard, bsg, bdf, bnd = (area(at + 3 * P * i, 3, P)[0:HA] for i in range(5))
        at += 15 * P
        qks = area(at, P)[0:HA]
        sel = area(at + P, HA, P)[0:HA]
        at = 2 * NQS_WORDS + 2 * TPC * CH - 2 * D
        gate = area(at, D)[0:E]
        bias1 = area(at + D, D)[0:1]
        scale_raw = area(TPC * CH, 2, D)[0:RS]
        scale_lo = area(TPC * CH + 2 * D, 2, D)[0:RS]
        cq_raw = area(WORK - G * P, G, P)[P - 4 * NFIX:P]
        kst = [kst_all[:, :, P * a * (a + 1):P * (a + 1) * (a + 2)] for a in range(NT // 2)]
        keys = pb[:, KEYS_AT, :, :].rearrange("p a b -> p (a b)")
        kv = pb[:, KEYS_AT - 1, 0, :]
        otS = xnT[:, 0:2, CH:T]
        attT = xnT[:, 2, CH:T]
        att = xnT[:, 3, CH:T]

        pair = [psum(f"pair{i}", [P, 2, CH]) for i in range(NPAIR)]
        aux = [psum(f"aux{i}", [P, CH]) for i in range(2)]

        w_in_sem = sem("w_in_sem")
        x_loaded = [sem(f"x_loaded{i}") for i in range(NT // 2)]
        bind_loaded = sem("bind_loaded")
        small_loaded = sem("small_loaded")
        big_loaded = sem("big_loaded")
        scales_loaded = sem("scales_loaded")
        cq_loaded = sem("cq_loaded")
        cq_ready = sem("cq_ready")
        scales_step = sem("scales_step")
        stored = [sem(f"stored{i}") for i in range(NT // 2)]
        const_ready = sem("const_ready")
        bind_step = sem("bind_step")
        setup_pe = sem("setup_pe")
        setup_out = sem("setup_out")
        bias_copied = sem("bias_copied")
        sign_ready = sem("sign_ready")
        pads_ready = sem("pads_ready")
        filled = sem("filled")
        act_took = sem("act_took")
        dve_took = sem("dve_took")
        took = {"act": act_took, "dve": dve_took}
        ln_stats = sem("ln_stats")
        ln_aggr = sem("ln_aggr")
        ln_var = sem("ln_var")
        ln_rstd = sem("ln_rstd")
        xn_ready = sem("xn_ready")
        va_ready = sem("va_ready")
        qT_ready = sem("qT_ready")
        aw_masked = sem("aw_masked")
        av_done = sem("av_done")
        xa_added = sem("xa_added")
        biased = sem("biased")
        soft_step = sem("soft_step")
        rt_split = sem("rt_split")
        exp_ready = sem("exp_ready")
        hi_ready = sem("hi_ready")
        lo_ready = sem("lo_ready")
        os_ready = sem("os_ready")
        xf_added = sem("xf_added")
        keys_step = sem("keys_step")
        key_scale_step = sem("key_scale_step")
        qT_split = sem("qT_split")
        kst_ready = sem("kst_ready")
        halves_zeroed = sem("halves_zeroed")
        stack_moved = [sem(f"stack_moved{i}") for i in range(NT // 2)]
        max_split = sem("max_split")
        max_ready = sem("max_ready")
        max_moved = [sem(f"max_moved{i}") for i in range(2)]
        pv_done = sem("pv_done")
        ot_ready = sem("ot_ready")
        rec_ready = sem("rec_ready")

        block = ctx.enter_context(nc.Block())

        def took_at(u):
            return took[u["who"]], u["order"]

        unit_of = {(u["kind"],) + u["args"]: u for u in units}

        def turned(b, l, t):
            return took_at(unit_of["turn", b, l, t - t % 2])

        def norm_T(l, c):
            return xnT_early if (l, c) == (1, 0) else xnT[:, :, c * CH:(c + 1) * CH]

        norm_order = {e[1:]: n for n, e in enumerate(e for e in events if e[0] == "norm")}
        stats_order = {e[1:]: n for n, e in enumerate(e for e in events if e[0] == "stats")}

        def normed(b, l, t):
            return norm_order[b, l, t // TPC] * TPC + t % TPC + 1

        def ffn_index(b, f, c):
            return (2 * b + f) * NC + c

        def tile_index(b, f, t):
            return (2 * b + f) * NT + t

        def last_max(b, qt):
            return unit_of["max", b, qt, qt // TPC, G - 1]

        def last_exp(b, qt):
            return unit_of["exp", b, qt, 1, qt, 1]

        exp_list = {b: [u for u in units if u["kind"] == "exp" and u["args"][0] == b] for b in range(B)}
        exp_index = {u["k"]: n for b in range(B) for n, u in enumerate(exp_list[b])}
        PV_PER = sum(2 * (q + 1) for q in range(NT))
        MASKS = TPC

        def pv_index(b, qt, half, kt):
            return b * PV_PER + qt * (qt + 1) + half * (qt + 1) + kt

        def diag_widths(c, i):
            return max(i * P - c * CH, 0)

        @block.sync
        def _(eng):
            xv = x_in.rearrange("b (t p) d -> b p t d", p=P)
            ov = out.rearrange("b (t p) d -> b p t d", p=P)

            def move_stack(b, a):
                if b == 0 and a == 0:
                    eng.wait_ge(cq_ready, 1)
                eng.wait_ge(*took_at(unit_of["q", b, a // 2, KT - 1]))
                if a >= NQS:
                    eng.wait_ge(filled, last_exp(b, 2 * (a - NQS) + 1)["k"] + 1)
                for j in range(2):
                    r = j * HP + R_SLOPE
                    for i in range(2):
                        at = (2 * i + j) * NFIX
                        eng.dma_start(qs_words[r:r + NFIX, a % NQS, :, i * P:(i + 1) * P],
                                      cq[at:at + NFIX, :, :].bitcast(F32)).then_inc(stack_moved[a], 16)
                lo = a % 2 * 2 * P
                for hh in range(8):
                    for part, q in enumerate((qT_hi[:, a // 2, :, :], qT_lo[a // 2], qT_hi[:, a // 2, :, :])):
                        r = hh % 2 * HP + part * DH
                        g = hh // 2 * GQ
                        eng.dma_start(qs_words[r:r + DH, a % NQS, g:g + GQ, :],
                                      q[hh * DH:(hh + 1) * DH, :, lo:lo + 2 * P].bitcast(F32)
                                      ).then_inc(stack_moved[a], 16)

            for t in range(0, NT, 2):
                eng.dma_start(x[:, t:t + 2, :], xv[0, :, t:t + 2, :]).then_inc(x_loaded[t // 2], 16)
            for e in events:
                if e[0] == "stack":
                    move_stack(*e[1:])
                elif e[0] == "store":
                    _, b, t = e
                    eng.wait_ge(xf_added, tile_index(b, 1, t + 1) + 1)
                    eng.dma_start(ov[b, :, t:t + 2, :], x[:, t:t + 2, :]).then_inc(stored[t // 2], 16)
                    if b + 1 < B:
                        eng.wait_ge(stored[t // 2], 16 * (b + 1))
                        eng.dma_start(x[:, t:t + 2, :], xv[b + 1, :, t:t + 2, :]).then_inc(x_loaded[t // 2], 16)
                elif e[0] == "unit" and e[1]["kind"] == "mt":
                    b, qt = e[1]["args"]
                    eng.wait_ge(*took_at(e[1]))
                    for j in range(2):
                        for n, m in enumerate((mT_hi, mT_lo)):
                            r = j * HP + R_MAX + n
                            eng.dma_start(qs_words[r:r + 1, qt // 2 % NQS, :, qt % 2 * P:(qt % 2 + 1) * P],
                                          m[j * G:(j + 1) * G, qt % 2, :].bitcast(F32)).then_inc(max_moved[qt % 2], 16)
            for done in stored:
                eng.wait_ge(done, 16 * B)

        @block.gpsimd
        def _(eng):
            eng.memset(ident[:, :], 0.0).then_inc(const_ready, 1)
            eng.memset(sel[:, :, :], 0.0).then_inc(const_ready, 1)
            eng.memset(negtri[:, :], 0.0).then_inc(const_ready, 1)
            eng.memset(negtriT[:, :], 0.0).then_inc(const_ready, 1)
            eng.memset(ones1[:, :], 1.0).then_inc(const_ready, 1)
            eng.memset(neghalf[:, :], -0.5).then_inc(const_ready, 1)
            eng.wait_ge(const_ready, 6)
            eng.affine_select(out=ident[:, :], in_=ident[:, :], compare_op=ALU.not_equal, fill=1.0,
                              base=0, pattern=[[-1, P]], channel_multiplier=1).then_inc(const_ready, 1)
            eng.affine_select(out=sel[:, :, :], in_=sel[:, :, :], compare_op=ALU.not_equal, fill=1.0,
                              base=0, pattern=[[-1, HA], [0, P]], channel_multiplier=1).then_inc(const_ready, 1)
            eng.affine_select(out=negtri[:, :], in_=negtri[:, :], compare_op=ALU.is_ge, fill=NEG,
                              base=0, pattern=[[-1, P]], channel_multiplier=1).then_inc(const_ready, 1)
            eng.affine_select(out=negtriT[:, :], in_=negtriT[:, :], compare_op=ALU.is_ge, fill=NEG,
                              base=0, pattern=[[1, P]], channel_multiplier=-1).then_inc(const_ready, 1)
            eng.wait_ge(const_ready, 10)
            eng.tensor_copy(identb[:, :], ident[:, :]).then_inc(const_ready, 1)
            eng.memset(rstk[:, :, :], 0.0).then_inc(pads_ready, 1)
            eng.memset(wk[:, :, :, :], 0.0).then_inc(pads_ready, 1)
            eng.memset(vb[:, :, :], 0.0).then_inc(pads_ready, 1)
            eng.wait_ge(pads_ready, 3)
            eng.memset(vb[:, :, DH:DH + 1], 1.0).then_inc(pads_ready, 1)
            eng.memset(scale_raw, 0.0).then_inc(pads_ready, 1)

            def pad_weights():
                eng.wait_ge(big_loaded, 16 * 11)
                for j in range(2):
                    for part in range(3):
                        eng.tensor_copy(wk[:, :, j, part * DH:(part + 1) * DH], wqkv[:, :, HB * DH:HB * DH + DH]
                                        ).then_inc(pads_ready, 1)
                eng.tensor_copy(wk[:, :, 0, R_VALUE:HP], wqkv[:, :, HB * DH + DH:]).then_inc(pads_ready, 1)

            def after_norm(b, l, c):
                n = norm_order[b, l, c]
                mine = slice(TPC * c, TPC * (c + 1))
                eng.wait_ge(ln_var, n + 1)
                eng.tensor_tensor(rstd[:, mine], ve[:, mine], neghalf[:, mine], ALU.pow).then_inc(ln_rstd, 1)
                for t in range(TPC):
                    tile = TPC * c + t
                    if l in (1, 3):
                        eng.wait_ge(bias_copied, 1)
                        eng.wait_ge(xn_ready, normed(b, l, tile))
                        eng.tensor_tensor(x[:, tile, :], x[:, tile, :], bias_bc[:, :], ALU.add).then_inc(biased, 1)

            def stage_a_values(b, c):
                eng.wait_ge(setup_out, 2)
                if b > 0 and c == 0:
                    eng.wait_ge(pv_done, b * PV_PER)
                for t in range(TPC * c, TPC * (c + 1)):
                    eng.wait_ge(xn_ready, normed(b, 0, t))
                    eng.tensor_tensor(va[:, t, :], xn[:, t, :], vbc[:, :], ALU.mult).then_inc(va_ready, 1)

            def mask(u):
                b, m, i0 = u["args"]
                c = m // HA
                for i in (i0, i0 + 1):
                    if i >= TPC * c:
                        w = diag_widths(c, i)
                        blk = aw[m % 2][:, i, w:w + P]
                        eng.wait_ge(*took_at(u))
                        eng.affine_select(out=blk, in_=blk, compare_op=ALU.is_ge, fill=0.0, base=0,
                                          pattern=[[1, P]], channel_multiplier=-1).then_inc(aw_masked, 1)

            def stack_keys(b, c):
                eng.wait_ge(keys_step, 5 * (b * NC + c + 1))
                eng.wait_ge(biased, NT * (2 * b + 1))
                for a in (2 * c, 2 * c + 1):
                    n_k = 2 * P * (a + 1)
                    for j in range(2):
                        r = j * HP
                        eng.tensor_tensor(kst[a][r:r + HP, j, :], keys[r:r + HP, 0:n_k], ramp[r:r + HP, T - n_k:T],
                                          ALU.add).then_inc(kst_ready, 1)
                eng.wait_ge(kst_ready, b * NT + (c + 1) * NT // 2)

            for e in events:
                if e[0] == "norm":
                    after_norm(*e[1:])
                elif e[0] == "va":
                    stage_a_values(*e[1:])
                    if e[1:] == (0, 1):
                        pad_weights()
                elif e[0] == "halves":
                    eng.wait_ge(*took_at(unit_of["wT", 0, 1]))
                    eng.wait_ge(aw_masked, MASKS * HA)
                    eng.memset(kst_all[HP:P, 0, :].bitcast(F32), 0.0).then_inc(halves_zeroed, 1)
                    eng.wait_ge(halves_zeroed, 1)
                    eng.memset(kst_all[0:HP, 1, :].bitcast(F32), 0.0).then_inc(halves_zeroed, 1)
                    eng.wait_ge(halves_zeroed, 2)
                elif e[0] == "unit" and e[1]["kind"] == "sig":
                    mask(e[1])
                elif e[0] == "unit" and e[1]["kind"] == "k":
                    stack_keys(*e[1]["args"])

        @block.scalar
        def _(eng):
            eng.dma_start(bv[:, 0, :], bv_q).then_inc(bind_loaded, 16)
            eng.dma_start(bv[:, 1, :], bv_k).then_inc(bind_loaded, 16)
            eng.dma_start(bv[:, 2, :], bv_v).then_inc(bind_loaded, 16)
            eng.dma_start(gate[:, :], gate_in).then_inc(small_loaded, 16)
            eng.dma_start(bias1[:, :], bias_in.rearrange("(a n) -> a n", a=1)).then_inc(small_loaded, 16)
            eng.wait_ge(pads_ready, 5)
            for r in (0, E, QR, QR + E):
                eng.dma_start(scale_raw[r:r + E, 0, :], ics_in).then_inc(scales_loaded, 16)
                eng.dma_start(scale_raw[r:r + E, 1, :], ocs_in).then_inc(scales_loaded, 16)
            eng.dma_start(cq_raw, cq_in).then_inc(cq_loaded, 16)
            eng.dma_start(wraw, w_in.rearrange("(o p) h -> p o h", p=P)).then_inc(w_in_sem, 16)
            for kt in range(KT):
                for half in range(2):
                    w = wqkv[:, kt, 0:HB * DH].rearrange("p (m h n) -> p m h n", m=KT, h=2)
                    eng.dma_start(w[:, :, half, :],
                                  wqkv_in[kt * P:(kt + 1) * P, half * D // 2:(half + 1) * D // 2]
                                  .rearrange("p (m n) -> p m n", m=KT)).then_inc(big_loaded, 16)
            eng.dma_start(wqkv[:, :, HB * DH:], wqkv_in.rearrange("(k p) n -> p k n", p=P)[:, :, HB * DH:]
                          ).then_inc(big_loaded, 16)
            eng.dma_start(wo[:, :, :], wo_in.rearrange("(k p) n -> p k n", p=P)).then_inc(big_loaded, 16)
            eng.dma_start(ramp[:, :], ramp_in).then_inc(big_loaded, 16)

            for e in events:
                if e[0] == "sign":
                    eng.wait_ge(w_in_sem, 16)
                    eng.activation(wsg, wraw, ACT.Sign).then_inc(sign_ready, 1)
                if e[0] == "soft":
                    _, b, f, c = e
                    mine = slice(TPC * c, TPC * (c + 1))
                    eng.wait_ge(*took_at(unit_of["logits", b, f, c]))
                    eng.activation(lexp[:, mine, :], lsub[:, mine, :], ACT.Exp).then_inc(exp_ready, 1)
                if e[0] == "pv":
                    _, b, qt, half, kt = e
                    if kt == qt:
                        eng.wait_ge(pv_done, pv_index(b, qt, half, kt) + 1)
                        if qt > 0:
                            eng.wait_ge(filled, unit_of["ot", b, qt - 1, half]["k"] + 1)
                        eng.activation(otS[:, half, :], aux[half][:, :], ACT.Copy).then_inc(ot_ready, 1)
                if e[0] != "unit":
                    continue
                u = e[1]
                kind, args, bank = u["kind"], u["args"], pair[u["slot"]]
                if kind in ("turn", "sig", "rT", "out", "q", "k", "v", "exp", "tt"):
                    eng.wait_ge(filled, u["k"] + 1)
                if kind == "turn":
                    _, l, t = args
                    at = t % TPC * P
                    eng.activation(norm_T(l, t // TPC)[:, :, at:at + 2 * P], bank[:, :, :].rearrange("p a (b q) -> p (a b) q", b=2),
                                   ACT.Copy).then_inc(act_took, 1)
                elif kind == "sig":
                    b, m, i = args
                    c = m // HA
                    if m >= 2 and i == 0:
                        eng.wait_ge(av_done, b * HA * NC + m - 1)
                    if i + 1 < TPC * c:
                        eng.activation(aw[m % 2][:, i:i + 2, :], bank[:, :, :], ACT.Sigmoid).then_inc(act_took, 1)
                    else:
                        w0, w1 = diag_widths(c, i), diag_widths(c, i + 1)
                        eng.activation(aw[m % 2][:, i, w0:CH], bank[:, 0, w0:CH], ACT.Sigmoid)
                        eng.activation(aw[m % 2][:, i + 1, w1:CH], bank[:, 1, w1:CH], ACT.Sigmoid).then_inc(act_took, 1)
                elif kind == "rT":
                    c = args[2]
                    eng.activation(rT[:, c * CH:(c + 1) * CH], bank[0:RS, 0, :], ACT.Copy).then_inc(act_took, 1)
                elif kind == "ins":
                    b, f, c, kp = args
                    eng.wait_ge(*took_at(u))
                    if c >= 1 and kp == 0:
                        eng.wait_ge(filled, unit_of["out", b, f, TPC * c - 1]["k"] + 1)
                    eng.activation(h_hi[:, 2 * kp:2 * kp + 2, :], hf[c][:, kp, :, :], ACT.Copy).then_inc(hi_ready, 1)
                elif kind == "out":
                    b, f, t = args
                    if t % TPC >= 2:
                        eng.wait_ge(xf_added, tile_index(b, f, t - 2) + 1)
                    eng.activation(osb[f][t // TPC][:, t % 2, :], bank[:, 1, :], ACT.Copy).then_inc(os_ready, 1)
                elif kind == "q":
                    b, c, k = args
                    eng.activation(qT_hi[:, c, k, :], bank[:, 0, :], ACT.Copy).then_inc(qT_split, 1)
                elif kind == "k":
                    b, c = args
                    if c > 0:
                        eng.wait_ge(filled, unit_of["v", b, c - 1]["k"] + 1)
                        eng.wait_ge(keys_step, 5 * (b * NC + c - 1) + 1)
                    eng.activation(kv, bank[:, 0, :], ACT.Copy).then_inc(act_took, 1)
                elif kind == "v":
                    b, c = args
                    eng.activation(vb[:, TPC * c:TPC * (c + 1), 0:DH],
                                   bank[:, 0, :].rearrange("p (t d) -> p t d", d=P)[:, :, R_VALUE:R_VALUE + DH],
                                   ACT.Copy).then_inc(act_took, 1)
                elif kind == "tt":
                    b, qt = args
                    if qt > 0:
                        eng.wait_ge(filled, unit_of["wo", b, qt - 1]["k"] + 1)
                    eng.activation(attT, bank[:, 0, :], ACT.Copy).then_inc(act_took, 1)
                elif kind == "exp":
                    b, n = args[0], exp_index[u["k"]]
                    if n == KEYS_AT:
                        eng.wait_ge(kst_ready, (b + 1) * NT)
                    if n in (NPB - 2, NPB - 1):
                        eng.wait_ge(stack_moved[0], 16 * 28 * (b + 1))
                        eng.wait_ge(stack_moved[1], 16 * 28 * (b + 1))
                    if n >= NPB:
                        _, qt, half, kt, _ = exp_list[b][n - NPB]["args"]
                        eng.wait_ge(pv_done, pv_index(b, qt, half, kt) + 1)
                    eng.activation(pb[:, n % NPB, :, :], bank[:, :, :], ACT.Exp).then_inc(act_took, 1)

        @block.tensor
        def _(eng):
            def room(u):
                if u["k"] >= NPAIR:
                    eng.wait_ge(*took_at(units[u["k"] - NPAIR]))

            eng.wait_ge(const_ready, 11)
            eng.wait_ge(bind_step, 7)
            eng.transpose(aux[0][:, 0:HA], qks[:, :], ident[0:HA, 0:HA]).then_inc(setup_pe, 1)
            for h in range(HA):
                mm = eng.matmul(aux[1][:, h * P:(h + 1) * P], sel[:, h, :], bnd[:, 2, :], start=True, stop=True)
            mm.then_inc(setup_pe, 1)
            def weigh(b, m):
                c, h = divmod(m, HA)
                n = b * HA * NC + m
                eng.wait_ge(*took_at(unit_of["sig", b, m, TPC * (c + 1) - 2]))
                eng.wait_ge(aw_masked, MASKS * (n + 1))
                eng.wait_ge(va_ready, NT * b + TPC * (c + 1))
                if m >= 2:
                    eng.wait_ge(xa_added, n - 1)
                elif b > 0:
                    eng.wait_ge(ot_ready, 2 * NT * b)
                for t in range(TPC * c, TPC * c + TPC):
                    lo = (t - TPC * c) * P
                    for i in range(t + 1):
                        mm = eng.matmul(aux[n % 2][:, lo:lo + P], aw[m % 2][:, i, lo:lo + P],
                                        va[:, i, h * P:(h + 1) * P], start=(i == 0), stop=(i == t))
                mm.then_inc(av_done, 1)

            def pv(b, qt, half, kt):
                if kt == 0 and qt * 2 + half >= 2:
                    eng.wait_ge(ot_ready, (b * NT + qt) * 2 + half - 1)
                for gp in range(2):
                    u = unit_of["exp", b, qt, half, kt, gp]
                    eng.wait_ge(*took_at(u))
                    for i in range(2):
                        j = 2 * gp + i
                        mm = eng.matmul(aux[half][j * QR:(j + 1) * QR, :], vb[:, kt, :],
                                        pb[:, exp_index[u["k"]] % NPB, i, :], start=(kt == 0), stop=(kt == qt),
                                        tile_position=(0, j * QR))
                mm.then_inc(pv_done, 1)

            for e in events:
                if e[0] == "weigh":
                    weigh(*e[1:])
                if e[0] == "pv":
                    pv(*e[1:])
                if e[0] != "unit":
                    continue
                u = e[1]
                kind, args, bank = u["kind"], u["args"], pair[u["slot"]]
                b = args[0]
                room(u)
                if kind == "small":
                    eng.wait_ge(small_loaded, 32)
                    eng.matmul(bank[:, 0, :], ones1[:, :], bias1[:, :], start=True, stop=True)
                    for kt in range(KT):
                        mm = eng.transpose(bank[:, 1, kt * E:(kt + 1) * E], gate[:, kt * P:(kt + 1) * P],
                                           ident[0:E, 0:E])
                elif kind == "wT":
                    _, kp = args
                    eng.wait_ge(sign_ready, 1)
                    for kt in (2 * kp, 2 * kp + 1):
                        for o in range(KT):
                            mm = eng.transpose(bank[:, kt % 2, o * P:(o + 1) * P], wsg[:, o, kt * P:(kt + 1) * P],
                                               ident[:, :])
                elif kind == "turn":
                    _, l, t0 = args
                    for t in (t0, t0 + 1):
                        eng.wait_ge(xn_ready, normed(b, l, t))
                        for kt in range(KT):
                            at = (kt % 2 * 2 + t - t0) * P
                            mm = eng.transpose(bank[:, kt // 2, at:at + P], xn[:, t, kt * P:(kt + 1) * P], ident[:, :])
                elif kind == "sig":
                    _, m, i0 = args
                    c, h = divmod(m, HA)
                    eng.wait_ge(qT_ready, (b * NC + c) * HA + h + 1)
                    for i in (i0, i0 + 1):
                        w = diag_widths(c, i)
                        mm = eng.matmul(bank[:, i - i0, w:CH], xnT[:, h, i * P:(i + 1) * P],
                                        qT[:, h, c * CH + w:(c + 1) * CH], start=True, stop=True)
                elif kind == "logits":
                    _, f, c = args
                    for t in range(TPC):
                        tile = TPC * c + t
                        eng.wait_ge(*turned(b, 2 * f + 1, tile))
                        for kt in range(KT):
                            mm = eng.matmul(bank[:, 0, t * E:(t + 1) * E], norm_T(2 * f + 1, c)[:, kt, t * P:(t + 1) * P],
                                            gateT[:, kt, :], start=(kt == 0), stop=(kt == KT - 1))
                elif kind == "rT":
                    _, f, c = args
                    eng.wait_ge(soft_step, 6 * ffn_index(b, f, c) + 6)
                    for t in range(TPC):
                        mm = eng.transpose(bank[0:RS, 0, t * P:(t + 1) * P], rstk[:, TPC * c + t, :], ident[:, :])
                elif kind == "ins":
                    _, f, c, kp = args
                    eng.wait_ge(*took_at(unit_of["rT", b, f, c]))
                    for i in range(2):
                        k = 2 * kp + i
                        mm = eng.matmul(bank[:, i, :], scales[:, 0, k * P:(k + 1) * P], rT[:, c * CH:(c + 1) * CH],
                                        start=True, stop=True)
                elif kind == "out":
                    _, f, t = args
                    eng.wait_ge(lo_ready, 2 * ffn_index(b, f, t // TPC) + 2)
                    eng.matmul(bank[:, 1, :], rT[:, t * P:(t + 1) * P], scales[:, 1, :], start=True, stop=True)
                    parts = [(h, kt) for h in (h_hi, h_lo) for kt in range(KT)]
                    for m, (h, kt) in enumerate(parts):
                        mm = eng.matmul(bank[:, 0, :], h[:, kt, t % TPC * P:(t % TPC + 1) * P], wT[:, kt, :],
                                        start=(m == 0), stop=(m == len(parts) - 1))
                elif kind == "q":
                    _, c, k = args
                    eng.wait_ge(pads_ready, 12)
                    eng.wait_ge(*turned(b, 2, TPC * c + TPC - 1))
                    for kt in range(KT):
                        mm = eng.matmul(bank[:, 0, :], wqkv[:, kt, k * P:(k + 1) * P], xnT[:, kt, c * CH:(c + 1) * CH],
                                        start=(kt == 0), stop=(kt == KT - 1))
                elif kind == "k":
                    _, c = args
                    for kt in range(KT):
                        mm = eng.matmul(bank[:, 0, :], wk[:, kt, :, :].rearrange("p j d -> p (j d)"),
                                        xnT[:, kt, c * CH:(c + 1) * CH], start=(kt == 0), stop=(kt == KT - 1))
                elif kind == "v":
                    _, c = args
                    eng.wait_ge(*took_at(unit_of["k", b, c]))
                    for t in range(TPC):
                        mm = eng.transpose(bank[:, 0, t * P:(t + 1) * P], kv[:, t * P:(t + 1) * P], ident[:, :])
                elif kind == "max":
                    _, qt, c, g = args
                    w = min(CH, (qt + 1) * P - c * CH)
                    diag = c == qt // TPC
                    eng.wait_ge(halves_zeroed, 2)
                    eng.wait_ge(kst_ready, b * NT + 2 * (qt // 2) + 2)
                    eng.wait_ge(stack_moved[qt // 2], 16 * 28 * (b + 1))
                    for i in range(2):
                        mm = eng.matmul(bank[:, i, 0:w], qs[:, qt // 2 % NQS, g, qt % 2 * P:(qt % 2 + 1) * P],
                                        kst[qt // 2][:, i, c * CH:c * CH + w], start=True, stop=not diag)
                    if diag:
                        for i in range(2):
                            mm = eng.matmul(bank[:, i, w - P:w], identb[:, :], negtri[:, :], start=False, stop=True)
                elif kind == "mt":
                    _, qt = args
                    if qt < TPC:
                        eng.wait_ge(*took_at(last_max(b, qt)))
                    else:
                        eng.wait_ge(max_ready, b * (NT - TPC) + qt - TPC + 1)
                    mm = eng.transpose(bank[0:HB, 0, 0:P], nmx[:, qt % 2, :], ident[:, :])
                elif kind == "exp":
                    _, qt, half, kt, gp = args
                    g = (2 * half + gp) * GQ
                    eng.wait_ge(max_moved[qt % 2], 16 * 4 * ((b * NT + qt) // 2 + 1))
                    eng.wait_ge(*took_at(unit_of["v", b, NC - 1]))
                    for i in range(2):
                        mm = eng.matmul(bank[:, i, :], kst[qt // 2][:, i, kt * P:(kt + 1) * P],
                                        qs[:, qt // 2 % NQS, g:g + GQ, qt % 2 * P:(qt % 2 + 1) * P],
                                        start=True, stop=kt < qt)
                    if kt == qt:
                        for i in range(2):
                            mm = eng.matmul(bank[:, i, :], identb[:, :],
                                            negtriT[:, :].unsqueeze(1).to_broadcast([P, GQ, P]),
                                            start=False, stop=True)
                elif kind == "ot":
                    _, qt, half = args
                    eng.wait_ge(ot_ready, (b * NT + qt) * 2 + half + 1)
                    for g in range(GQ):
                        mm = eng.transpose(bank[:, 0, g * P:(g + 1) * P], otS[:, half, g * P:(g + 1) * P], ident[:, :])
                elif kind == "tt":
                    _, qt = args
                    eng.wait_ge(*took_at(unit_of["ot", b, qt, 1]))
                    for kt in range(KT):
                        mm = eng.transpose(bank[:, 0, kt * P:(kt + 1) * P], att[:, kt * P:(kt + 1) * P], ident[:, :])
                elif kind == "wo":
                    _, qt = args
                    eng.wait_ge(*took_at(unit_of["tt", b, qt]))
                    for kt in range(KT):
                        mm = eng.matmul(bank[:, 0, :], attT[:, kt * P:(kt + 1) * P], wo[:, kt, :],
                                        start=(kt == 0), stop=(kt == KT - 1))
                mm.then_inc(filled, 1)

        @block.vector
        def _(eng):
            eng.wait_ge(bind_loaded, 48)
            eng.tensor_reduce(alpha[:, :], bv[:, :, :], AX.X, ALU.add, apply_absolute_value=True).then_inc(bind_step, 1)
            eng.tensor_scalar(bsg[:, :, :], bv[:, :, :], 0.0, 2.0, ALU.is_ge, ALU.mult).then_inc(bind_step, 1)
            eng.wait_ge(bind_step, 2)
            eng.tensor_scalar(alpham[:, :], alpha[:, :], 1.0 / P, None, ALU.mult).then_inc(bind_step, 1)
            eng.wait_ge(bind_step, 3)
            eng.scalar_tensor_tensor(out=hard[:, :, :], in0=bsg[:, :, :], scalar=-1.0,
                                     in1=alpham[:, :].unsqueeze(2).to_broadcast([HA, 3, P]),
                                     op0=ALU.add, op1=ALU.mult).then_inc(bind_step, 1)
            eng.wait_ge(bind_step, 4)
            eng.tensor_tensor(bdf[:, :, :], hard[:, :, :], bv[:, :, :], ALU.subtract).then_inc(bind_step, 1)
            eng.wait_ge(bind_step, 5)
            eng.tensor_tensor(bnd[:, :, :], bdf[:, :, :], bv[:, :, :], ALU.add).then_inc(bind_step, 1)
            eng.wait_ge(bind_step, 6)
            eng.scalar_tensor_tensor(out=qks[:, :], in0=bnd[:, 0, :], scalar=4.0 * float(P) ** -0.5,
                                     in1=bnd[:, 1, :], op0=ALU.mult, op1=ALU.mult).then_inc(bind_step, 1)
            eng.wait_ge(setup_pe, 1)
            eng.tensor_copy(wqk[:, :], aux[0][:, 0:HA]).then_inc(setup_out, 1)
            eng.wait_ge(setup_pe, 2)
            eng.tensor_copy(vbc[:, :], aux[1][:, :]).then_inc(setup_out, 1)
            eng.wait_ge(const_ready, 11)
            eng.tensor_reduce(key_scale[:, 1:2], ident[:, R_VALUE:HP], AX.X, ALU.add).then_inc(key_scale_step, 1)
            eng.wait_ge(key_scale_step, 1)
            eng.tensor_scalar(key_scale[:, 0:1], key_scale[:, 1:2], -float(DH) ** -0.5, float(DH) ** -0.5,
                              ALU.mult, ALU.add).then_inc(key_scale_step, 1)

            def channel_scales():
                eng.wait_ge(scales_loaded, 128)
                eng.tensor_copy(scales[:, :, :], scale_raw).then_inc(scales_step, 1)
                eng.wait_ge(cq_loaded, 16)
                eng.tensor_copy(cq[:, :, :], cq_raw).then_inc(cq_ready, 1)
                eng.wait_ge(scales_step, 1)
                eng.tensor_tensor(scale_lo[QR:RS], scale_raw[QR:RS], scales[QR:RS, :, :].bitcast(F32), ALU.subtract
                                  ).then_inc(scales_step, 1)
                eng.wait_ge(scales_step, 2)
                eng.tensor_copy(scales[QR:RS, :, :], scale_lo[QR:RS]).then_inc(scales_step, 1)

            def tile_ready(b, l, t):
                if l == 0:
                    eng.wait_ge(x_loaded[t // 2], 16 * (b + 1))
                elif l == 1:
                    eng.wait_ge(xa_added, b * HA * NC + HA * (t // TPC + 1))
                elif l == 2:
                    eng.wait_ge(xf_added, tile_index(b, 0, t) + 1)
                else:
                    eng.wait_ge(*took_at(unit_of["wo", b, t]))

            def norm(b, l, c):
                n = norm_order[b, l, c]
                tiles = range(TPC * c, TPC * (c + 1))
                mine = slice(TPC * c, TPC * (c + 1))
                for t in tiles:
                    eng.wait_ge(ln_stats, stats_order[b, l, t] + 1)
                    eng.bn_aggr(mv[:, t, :], st[:, t, :]).then_inc(ln_aggr, 1)
                eng.wait_ge(ln_aggr, (n + 1) * TPC)
                eng.tensor_scalar(ve[:, mine], mv[:, mine, 1], EPS, None, ALU.add).then_inc(ln_var, 1)
                if l == 3:
                    for a in (2 * c, 2 * c + 1):
                        eng.wait_ge(stack_moved[a], 16 * 28 * (b + 1))
                eng.wait_ge(ln_rstd, n + 1)
                for t in tiles:
                    eng.tensor_scalar(xn[:, t, :], x[:, t, :], mv[:, t, 0:1], rstd[:, t:t + 1],
                                      ALU.subtract, ALU.mult).then_inc(xn_ready, 1)

            def route(b, f, c):
                n = ffn_index(b, f, c)
                mine = slice(TPC * c, TPC * (c + 1))
                eng.wait_ge(exp_ready, n + 1)
                eng.tensor_reduce(lsum[:, mine], lexp[:, mine, :], AX.X, ALU.add).then_inc(soft_step, 1)
                eng.wait_ge(soft_step, 6 * n + 2)
                eng.reciprocal(lrec[:, mine], lsum[:, mine]).then_inc(soft_step, 1)
                eng.wait_ge(soft_step, 6 * n + 3)
                eng.tensor_tensor(rt[:, mine, :], lexp[:, mine, :],
                                  lrec[:, mine].unsqueeze(2).to_broadcast([P, TPC, E]), ALU.mult).then_inc(soft_step, 1)
                eng.wait_ge(soft_step, 6 * n + 4)
                eng.tensor_copy(rt_hi[:, mine, :], rt[:, mine, :]).then_inc(rt_split, 1)
                eng.wait_ge(rt_split, n + 1)
                places = rstk[:, mine, :].rearrange("p t (a e) -> p t a e", a=2)
                both = [P, TPC, 2, E]
                hi = rt_hi[:, mine, :].bitcast(F32).unsqueeze(2).to_broadcast(both)
                eng.tensor_copy(places[:, :, :, 0:E], hi).then_inc(soft_step, 1)
                eng.tensor_tensor(places[:, :, :, E:2 * E], rt[:, mine, :].unsqueeze(2).to_broadcast(both), hi,
                                  ALU.subtract).then_inc(soft_step, 1)

            for e in events:
                if e[0] == "channel_scales":
                    channel_scales()
                if e[0] == "stats":
                    _, b, l, t = e
                    tile_ready(b, l, t)
                    eng.bn_stats(st[:, t, :], x[:, t, :]).then_inc(ln_stats, 1)
                elif e[0] == "norm":
                    norm(*e[1:])
                elif e[0] == "qT":
                    _, b, c = e
                    eng.wait_ge(*turned(b, 0, TPC * c + TPC - 1))
                    for h in range(HA):
                        eng.tensor_scalar(qT[:, h, c * CH:(c + 1) * CH], xnT[:, h, c * CH:(c + 1) * CH],
                                          wqk[:, h:h + 1], None, ALU.mult).then_inc(qT_ready, 1)
                elif e[0] == "weigh":
                    _, b, m = e
                    c, h = divmod(m, HA)
                    n = b * HA * NC + m
                    xs = x[:, TPC * c:TPC * c + TPC, h * P:(h + 1) * P]
                    eng.wait_ge(av_done, n + 1)
                    eng.tensor_tensor(xs, aux[n % 2][:, :].rearrange("p (t q) -> p t q", q=P), xs, ALU.add
                                      ).then_inc(xa_added, 1)
                elif e[0] == "soft":
                    route(*e[1:])
                if e[0] != "unit":
                    continue
                u = e[1]
                kind, args, bank = u["kind"], u["args"], pair[u["slot"]]
                b = args[0]
                if kind in ("small", "wT", "logits", "ins", "max", "mt", "ot", "wo"):
                    eng.wait_ge(filled, u["k"] + 1)
                if kind == "small":
                    eng.tensor_copy(bias_bc[:, :], bank[:, 0, :]).then_inc(bias_copied, 1)
                    eng.tensor_copy(gateT[:, :, :], bank[:, 1, 0:KT * E].rearrange("p (k e) -> p k e", e=E)
                                    ).then_inc(dve_took, 1)
                elif kind == "wT":
                    _, kp = args
                    eng.tensor_copy(wT[:, 2 * kp:2 * kp + 2, :], bank[:, :, :]).then_inc(dve_took, 1)
                elif kind == "logits":
                    _, f, c = args
                    mine = slice(TPC * c, TPC * (c + 1))
                    lg = bank[:, 0, 0:TPC * E].rearrange("p (t e) -> p t e", e=E)
                    eng.tensor_reduce(lmax[:, mine], lg, AX.X, ALU.max).then_inc(soft_step, 1)
                    eng.wait_ge(soft_step, 6 * ffn_index(b, f, c) + 1)
                    eng.tensor_tensor(lsub[:, mine, :], lg, lmax[:, mine].unsqueeze(2).to_broadcast([P, TPC, E]),
                                      ALU.subtract).then_inc(dve_took, 1)
                elif kind == "ins":
                    _, f, c, kp = args
                    if f == 1 and c == 0 and kp == 0:
                        for a in range(NT // 2):
                            eng.wait_ge(stack_moved[a], 16 * 28 * (b + 1))
                    eng.tensor_tensor(hf[c][:, kp, :, :], bank[:, :, :],
                                      norm_T(2 * f + 1, c)[:, 2 * kp:2 * kp + 2, :], ALU.mult).then_inc(dve_took, 1)
                    eng.wait_ge(hi_ready, 2 * ffn_index(b, f, c) + kp + 1)
                    eng.tensor_tensor(h_lo[:, 2 * kp:2 * kp + 2, :], hf[c][:, kp, :, :],
                                      h_hi[:, 2 * kp:2 * kp + 2, :].bitcast(F32), ALU.subtract).then_inc(lo_ready, 1)
                elif kind == "out":
                    _, f, t = args
                    n = tile_index(b, f, t)
                    o = osb[f][t // TPC][:, t % 2, :]
                    eng.wait_ge(os_ready, n + 1)
                    eng.tensor_tensor(o, bank[:, 0, :], o, ALU.mult).then_inc(dve_took, 1)
                    eng.wait_ge(*took_at(u))
                    eng.wait_ge(biased, n + 1)
                    eng.tensor_tensor(x[:, t, :], o, x[:, t, :], ALU.add).then_inc(xf_added, 1)
                elif kind == "q":
                    _, c, k = args
                    eng.wait_ge(qT_split, (b * NC + c) * KT + k + 1)
                    eng.tensor_tensor(qT_lo[c][:, k, :], bank[:, 0, :], qT_hi[:, c, k, :].bitcast(F32), ALU.subtract
                                      ).then_inc(dve_took, 1)
                elif kind == "k":
                    _, c = args
                    eng.wait_ge(key_scale_step, 2)
                    cols = slice(c * CH, (c + 1) * CH)
                    eng.wait_ge(*took_at(u))
                    eng.tensor_scalar(keys[:, cols], kv, key_scale[:, 0:1], None, ALU.mult).then_inc(keys_step, 1)
                    eng.wait_ge(keys_step, 5 * (b * NC + c) + 1)
                    for n, r in enumerate((QR, HP + QR)):
                        eng.tensor_copy(kst[-1][r:r + DH, n, cols], keys[r:r + DH, cols]).then_inc(keys_step, 1)
                        eng.wait_ge(keys_step, 5 * (b * NC + c) + 2 * n + 2)
                        eng.tensor_tensor(keys[r:r + DH, cols], keys[r:r + DH, cols],
                                          kst[-1][r:r + DH, n, cols].bitcast(F32), ALU.subtract).then_inc(keys_step, 1)
                elif kind == "max":
                    _, qt, c, g = args
                    w = min(CH, (qt + 1) * P - c * CH)
                    o = mx[:, qt % 2, c, :] if qt >= TPC else nmx[:, qt % 2, :]
                    if 2 <= qt < TPC and g == 0:
                        eng.wait_ge(filled, unit_of["mt", b, qt - 2]["k"] + 1)
                    o = o.rearrange("p (j g) -> p j g", j=2)[:, :, g]
                    eng.tensor_reduce(o, bank[:, :, 0:w], AX.X, ALU.max, negate=True).then_inc(dve_took, 1)
                    if c == qt // TPC and g == G - 1 and qt >= TPC:
                        eng.wait_ge(*took_at(u))
                        eng.wait_ge(filled, unit_of["mt", b, qt - 2]["k"] + 1)
                        eng.tensor_tensor(nmx[:, qt % 2, :], mx[:, qt % 2, 0, :], mx[:, qt % 2, 1, :], ALU.min
                                          ).then_inc(max_ready, 1)
                elif kind == "mt":
                    _, qt = args
                    if qt >= 2 or b > 0:
                        eng.wait_ge(max_moved[qt % 2], 16 * 4 * ((b * NT + qt) // 2))
                    eng.tensor_copy(mT_hi[:, qt % 2, :], bank[0:HB, 0, 0:P]).then_inc(max_split, 1)
                    eng.wait_ge(max_split, b * NT + qt + 1)
                    eng.tensor_tensor(mT_lo[:, qt % 2, :], bank[0:HB, 0, 0:P], mT_hi[:, qt % 2, :].bitcast(F32),
                                      ALU.subtract).then_inc(dve_took, 1)
                elif kind == "ot":
                    _, qt, half = args
                    o = bank[:, 0, :].rearrange("p (h d) -> p h d", d=QR)
                    eng.reciprocal(rec[:, half, :].unsqueeze(2), o[:, :, DH:DH + 1]).then_inc(rec_ready, 1)
                    eng.wait_ge(rec_ready, (b * NT + qt) * 2 + half + 1)
                    if qt > 0 and half == 0:
                        eng.wait_ge(filled, unit_of["tt", b, qt - 1]["k"] + 1)
                    eng.tensor_tensor(att[:, half * D // 2:(half + 1) * D // 2].rearrange("p (h d) -> p h d", d=DH),
                                      o[:, :, 0:DH], rec[:, half, :].unsqueeze(2).to_broadcast([P, HB // 2, DH]),
                                      ALU.mult).then_inc(dve_took, 1)
                elif kind == "wo":
                    _, qt = args
                    eng.tensor_tensor(x[:, qt, :], bank[:, 0, :], x[:, qt, :], ALU.add).then_inc(dve_took, 1)


def split12(v):
    hi = (((v.view(np.uint32) + np.uint32(0x800)) >> np.uint32(12)) << np.uint32(12)).view(np.float32)
    return hi, v - hi


def constants():
    base = 2.0 ** (-2.0 ** (-(np.log2(HB) - 3)))
    slope = (base ** np.arange(1, HB + 1, dtype=np.float64)).astype(np.float32)
    cq = np.zeros((2, 2, NFIX, G, P), np.float32)
    ramp = np.zeros((P, T), np.float32)
    for j in range(2):
        for g in range(G):
            half, gp, g4 = g // 8, g // 4 % 2, g % 4
            s = slope[16 * half + 4 * g4 + 2 * gp + j]
            for a in range(2):
                cq[a, j, 0, g, :], cq[a, j, 1, g, :] = split12(np.full(P, s, np.float32))
                off = (-s.astype(np.float64) * (a * P + np.arange(P))).astype(np.float32)
                cq[a, j, 2, g, :], cq[a, j, 3, g, :] = split12(off)
        ramp[j * HP + R_SLOPE:j * HP + R_OFF, :] = np.arange(T) - (T - 2 * P)
        ramp[j * HP + R_OFF:j * HP + R_MAX + 2, :] = 1.0
    cq = cq.reshape(4 * NFIX, G, P)
    return cq, ramp


_INS = ["L0_attn_a_x", "L0_attn_a_bv_q", "L0_attn_a_bv_k", "L0_attn_a_bv_v", "L0_attn_b_Wqkv", "L0_attn_b_Wo",
        "L0_ffn_weight", "L0_ffn_bias", "L0_ffn_gate_w", "L0_ffn_in_channel_scale", "L0_ffn_out_channel_scale"]


def kernel(**inputs):
    import concourse.bacc as _bacc
    from concourse.bass_utils import run_bass_kernel_spmd as _run

    nc = _bacc.Bacc("TRN2", target_bir_lowering=False, num_devices=1)
    arrays = {f"in_{n}_dram": np.ascontiguousarray(inputs[n]) for n in _INS}
    cq, ramp = constants()
    arrays["slope_rows_dram"], arrays["position_rows_dram"] = cq, ramp
    args = [nc.dram_tensor(n, a.shape, mybir.dt.from_np(a.dtype), kind="ExternalInput").ap() for n, a in arrays.items()]
    out = nc.dram_tensor("out_0_dram", (B, T, D), F32, kind="ExternalOutput").ap()
    build(nc, *args, out)
    r = _run(nc, [arrays], core_ids=[0])
    return r.results[0]["out_0_dram"]
```
